# Optimizing a Trainium2 kernel written in Bass

```python
import numpy as np
import jax
import jax.numpy as jnp

def _softmax(x, axis=-1):
    return jax.nn.softmax(x, axis=axis)
def _gelu(x):
    return jax.nn.gelu(x, approximate=True)
def _silu(x):
    return jax.nn.silu(x)
def _sigmoid(x):
    return jax.nn.sigmoid(x)
def _layernorm(x, axis=-1, eps=1e-5):
    m = jnp.mean(x, axis=axis, keepdims=True)
    v = jnp.var(x, axis=axis, keepdims=True)
    return (x - m) / jnp.sqrt(v + eps)
def _scatter_add(tgt, idx, src, axis=0):
    return tgt.at[idx].add(src)
def _segment_sum(src, seg, n):
    return jax.ops.segment_sum(src, seg, n)

kernel_name = 'mk_conv_seq_d1_conv_nhwc768_1cf10e'

def setup_inputs(seed: int = 0):
    np.random.seed(seed)
    _w = jnp.asarray
    def _rec_inputs():
        import jax
        import jax.numpy as jnp
        _gk = jax.random.key(seed)
        x = -4.65e-05 + 0.9999 * jax.random.normal(jax.random.fold_in(_gk, 1), (1, 256, 256, 768), jnp.float32)
        return x
    x = _rec_inputs()
    def _L0_conv_setup():
        import jax, jax.numpy as jnp
        import numpy as np
        SPARSITY_THRESHOLD = 0.01
        HARD_THRESH_FRAC = 1.0

        def softshrink(x, lam):
            return jnp.where(x > lam, x - lam, jnp.where(x < -lam, x + lam, jnp.zeros_like(x)))

        def compl_mul_add_act(a, b, c):
            tmp = jnp.einsum('bxykis,kiot->stbxyko', a, b)
            real = tmp[0, 0] - tmp[1, 1]
            imag = tmp[1, 0] + tmp[0, 1]
            return jnp.stack([real, imag], axis=-1) + c
        key = jax.random.key(seed)
        k = jax.random.split(key, 5)
        B, H, W, C = (1, 256, 256, 768)
        nb, bs, factor = (8, 96, 1)
        scale = 0.02
        return {'x': jax.random.normal(k[0], (B, H, W, C), dtype=jnp.float32), 'w1': scale * jax.random.normal(k[1], (nb, bs, bs * factor, 2), dtype=jnp.float32), 'b1': scale * jax.random.normal(k[2], (nb, bs * factor, 2), dtype=jnp.float32), 'w2': scale * jax.random.normal(k[3], (nb, bs * factor, bs, 2), dtype=jnp.float32), 'b2': scale * jax.random.normal(k[4], (nb, bs, 2), dtype=jnp.float32)}
    _L0_conv_all = _L0_conv_setup()
    _L0_conv_in = {k: v for k, v in _L0_conv_all.items() if k in ('w1', 'b1', 'w2', 'b2', )}
    del _L0_conv_all

    return {
        "x": x,
        "L0_conv_w1": _L0_conv_in["w1"],
        "L0_conv_b1": _L0_conv_in["b1"],
        "L0_conv_w2": _L0_conv_in["w2"],
        "L0_conv_b2": _L0_conv_in["b2"],
    }

def reference(x, L0_conv_w1, L0_conv_b1, L0_conv_w2, L0_conv_b2):
    import jax
    import jax.numpy as jnp
    def _L0_conv_ref(x, w1, b1, w2, b2):
        import jax, jax.numpy as jnp
        import numpy as np
        SPARSITY_THRESHOLD = 0.01
        HARD_THRESH_FRAC = 1.0

        def softshrink(x, lam):
            return jnp.where(x > lam, x - lam, jnp.where(x < -lam, x + lam, jnp.zeros_like(x)))

        def compl_mul_add_act(a, b, c):
            tmp = jnp.einsum('bxykis,kiot->stbxyko', a, b)
            real = tmp[0, 0] - tmp[1, 1]
            imag = tmp[1, 0] + tmp[0, 1]
            return jnp.stack([real, imag], axis=-1) + c
        bias = x
        dtype = x.dtype
        B, H, W, C = x.shape
        nb, bs = (w1.shape[0], w1.shape[1])
        total_modes = H // 2 + 1
        kept_modes = int(total_modes * HARD_THRESH_FRAC)
        lo = total_modes - kept_modes
        hi = min(total_modes + kept_modes, H)
        xf = jnp.fft.rfft2(x.astype(jnp.float32), axes=(1, 2), norm='ortho')
        xf = xf.reshape(B, H, W // 2 + 1, nb, bs)
        xs = jnp.stack([xf.real, xf.imag], axis=-1)
        sub = xs[:, lo:hi, :kept_modes]
        o1 = jax.nn.relu(compl_mul_add_act(sub, w1, b1))
        o2 = jnp.zeros_like(xs).at[:, lo:hi, :kept_modes].set(compl_mul_add_act(o1, w2, b2))
        o2 = softshrink(o2, SPARSITY_THRESHOLD)
        xc = (o2[..., 0] + 1j * o2[..., 1]).reshape(B, H, W // 2 + 1, C)
        out = jnp.fft.irfft2(xc, s=(H, W), axes=(1, 2), norm='ortho').astype(dtype)
        return out + bias

    def _gn(v, G=32, eps=1e-5):
        B_, H_, W_, C_ = v.shape
        g = v.reshape(B_, H_, W_, G, C_ // G)
        m = jnp.mean(g, axis=(1, 2, 4), keepdims=True)
        s = jnp.var(g, axis=(1, 2, 4), keepdims=True)
        return ((g - m) / jnp.sqrt(s + eps)).reshape(v.shape)

    def _ln_c(v, eps=1e-6):
        m = jnp.mean(v, axis=-1, keepdims=True)
        s = jnp.var(v, axis=-1, keepdims=True)
        return (v - m) / jnp.sqrt(s + eps)

    def _ln_t(v, eps=1e-5):
        m = jnp.mean(v, axis=-1, keepdims=True)
        s = jnp.var(v, axis=-1, keepdims=True)
        return (v - m) / jnp.sqrt(s + eps)

    def _to_tokens(v):
        B_, H_, W_, C_ = v.shape
        return v.reshape(B_, H_ * W_, C_)
    def _from_tokens(t, like):
        return t.reshape(like.shape)

    x = _L0_conv_ref(x, L0_conv_w1, L0_conv_b1, L0_conv_w2, L0_conv_b2)
    return x


_drawn_inputs = setup_inputs


def setup_inputs(seed=0):
    import zlib

    import numpy as np

    out = dict(_drawn_inputs(seed))
    spreads = {}
    factors = {'L0_conv_b1': 8.0}
    for name, (base, spread) in spreads.items():
        noise = np.random.default_rng([zlib.crc32(name.encode()), seed]).standard_normal(out[name].shape)
        drawn = base * np.exp(spread * noise) if base else spread * noise
        out[name] = jnp.asarray(drawn.astype(out[name].dtype))
    for name, factor in factors.items():
        out[name] = (out[name] * factor).astype(out[name].dtype)
    return out
```

```python
from contextlib import ExitStack

import numpy as np

import concourse.bass as bass
from concourse import mybir

ALU = mybir.AluOpType
ACT = mybir.ActivationFunctionType
F32 = mybir.dt.float32
F32R = mybir.dt.float32r

LAMBDA = float(np.float32(0.01))
SIDE = 256
HALF = SIDE // 2
CHANNELS = 768
BLOCK = 96
GROUPS = 2
GC = CHANNELS // GROUPS
BLOCKS = GC // BLOCK
KX = HALF + 1
UNITS = GROUPS * KX
STEPS = UNITS * BLOCKS
ROWS = GROUPS * HALF
PITCH = HALF * 2 * GC + 1024
LEAD = 4
INV_AT = KX + 4
DMA = 16


class Index:

    def __init__(self, first, reg=None):
        self.first, self.reg, self.slot = first, reg, first % 2

    def count(self, times=1, plus=0):
        value = times * self.first + plus
        return value if self.reg is None else self.reg * (2 * times) + value

    def uses(self, plus=0, dmas=2):
        value = dmas * DMA * (self.first // 2 + plus)
        return value if self.reg is None else self.reg * (dmas * DMA) + value

    def __add__(self, n):
        return Index(self.first + n, self.reg)


def group_of(unit):
    return 0 if unit < KX else 1


def spectral_conv(nc, x, w1, b1, w2, b2, fwd_w, inv_w, fwd_h, inv_h, out):
    s1 = nc.dram_tensor("s1_scratch", (GROUPS, 2, HALF, PITCH), F32, kind="Internal").ap()
    s2 = nc.dram_tensor("s2_scratch", (GROUPS, 2, HALF, PITCH), F32, kind="Internal").ap()

    with ExitStack() as ctx:
        def sb(name, shape, dt=F32):
            return ctx.enter_context(nc.sbuf_tensor(name, shape, dt))

        def ps(name):
            return ctx.enter_context(nc.psum_tensor(name, [128, 512], F32))

        def sem(name):
            return ctx.enter_context(nc.semaphore(name))

        xt = sb("xt", [128, 2, 2, 2, GC])
        hfold = sb("hfold", [128, 2, 2, GC])
        wmov = sb("wmov", [128, 2, 2, 2, GC])
        wout = sb("wout", [128, 2, 2, 2, GC])
        fw = sb("fw", [128, 2, 128])
        iw = sb("iw", [128, 2, 128])
        sin = sb("sin", [128, 2, 2, 2, GC])
        sin_hi = sb("sin_hi", [128, 2, 2, 2, GC], F32R)
        sin_lo = sb("sin_lo", [128, 2, 2, 2, GC], F32R)
        spec_hi = sb("spec_hi", [BLOCK + 1, 2, 2, SIDE], F32R)
        spec_lo = sb("spec_lo", [BLOCK, 2, 2, SIDE], F32R)
        hid_hi = sb("hid_hi", [BLOCK + 1, 2, 2, SIDE], F32R)
        hid_lo = sb("hid_lo", [BLOCK, 2, 2, SIDE], F32R)
        above = sb("above", [128, 2, 2, 2, BLOCK])
        shrunk = sb("shrunk", [128, 2, 2, 2, BLOCK])
        shr_hi = sb("shr_hi", [128, 2, 2, BLOCKS, 2, BLOCK], F32R)
        shr_lo = sb("shr_lo", [128, 2, 2, BLOCKS, 2, BLOCK], F32R)
        evens = sb("evens", [128, 2, GC])
        sout = sb("sout", [128, 2, 2, 2, GC])
        fh = sb("fh", [128, 2, 2, 3, 128], F32R)
        ih = sb("ih", [128, 2, 2, 3, 128], F32R)
        m1 = sb("m1", [BLOCK + 1, 2, 8, 3, BLOCK], F32R)
        m2 = sb("m2", [BLOCK + 1, 2, 8, 3, BLOCK], F32R)
        minus2l = sb("minus2l", [128, 1])

        h_bank = [ps("h_bank0"), ps("h_bank1")]
        l1_bank, l2_bank = ps("l1_bank"), ps("l2_bank")
        ih_bank = [ps("ih_even"), ps("ih_odd")]
        w_bank = [ps("w_bank0"), ps("w_bank1")]

        wconst_in = sem("wconst_in")
        hconst_in = sem("hconst_in")
        mlp_in = sem("mlp_in")
        prepared = sem("prepared")
        x_in = [sem("x_in0"), sem("x_in1")]
        hsum_done = sem("hsum_done")
        hdif_done = sem("hdif_done")
        folded = sem("folded")
        fwd_mm = sem("fwd_mm")
        fwd_out = sem("fwd_out")
        s1_put = [sem("s1_put0"), sem("s1_put1")]
        sin_in = [sem("sin_in0"), sem("sin_in1")]
        sin_hi_done, sin_lo_done = sem("sin_hi_done"), sem("sin_lo_done")
        h_mm = sem("h_mm")
        spec_hi_done, spec_lo_done = sem("spec_hi_done"), sem("spec_lo_done")
        l1_mm = sem("l1_mm")
        hid_hi_done, hid_lo_done = sem("hid_hi_done"), sem("hid_lo_done")
        l2_mm = sem("l2_mm")
        above_done = sem("above_done")
        shrunk_done = sem("shrunk_done")
        shr_hi_done, shr_lo_done = sem("shr_hi_done"), sem("shr_lo_done")
        ihe_mm, iho_mm = sem("ihe_mm"), sem("iho_mm")
        evens_done = sem("evens_done")
        sout_done = sem("sout_done")
        s2_put = [sem("s2_put0"), sem("s2_put1")]
        xr_in = [sem("xr_in0"), sem("xr_in1")]
        wsp_in = [sem("wsp_in0"), sem("wsp_in1")]
        inv_mm = sem("inv_mm")
        inv_out = sem("inv_out")
        y_put = [sem("y_put0"), sem("y_put1")]

        raw_h = sin[:, :, :, :, :].rearrange("p s a b c -> p s (a b c)")
        raw_m = sout[:, :, :, :, :].rearrange("p s a b c -> p s (a b c)")

        def rows_of(scratch, g, t, q):
            return scratch[g, t, q, 0:HALF * 2 * GC].rearrange("(h c) -> h c", h=HALF)

        def packed_rows(scratch, g, t, h):
            return scratch[g, t].rearrange("(o k) c -> k o c", o=2)[:, :, bass.ts(h, 2 * GC)]

        def image(a, g, h, hh):
            row = a[0, HALF * hh:HALF * (hh + 1)][h]
            return row.rearrange("(v w) c -> w v c", v=2)[:, :, g * GC:(g + 1) * GC]

        def h_of(k):
            return k.count(1, -HALF * (k.first // HALF))

        block = ctx.enter_context(nc.Block())

        @block.sync
        def _(sp):
            def load_x(k, landed):
                for hh in range(2):
                    sp.dma_start(xt[:, k.slot, hh], image(x, k.first // HALF, h_of(k), hh)) \
                        .then_inc(landed[k.slot], DMA)

            def fwd_unit(k):
                if k.first + 2 < ROWS:
                    sp.wait_ge(hsum_done, k.count(1, 1))
                    sp.wait_ge(hdif_done, k.count(1, 1))
                    load_x(k + 2, x_in)
                if k.first >= 1:
                    store_s1(k + -1)

            def store_s1(k):
                sp.wait_ge(fwd_out, k.count(4, 4))
                for t in range(2):
                    sp.dma_start(packed_rows(s1, k.first // HALF, t, h_of(k)),
                                 wout[64 * t:64 * t + 64, k.slot].rearrange("p o e c -> p o (e c)")) \
                        .then_inc(s1_put[k.slot], DMA)

            def load_sin(u):
                g = group_of(u.first)
                v = u.first - KX * g
                for t in range(2):
                    row = rows_of(s1, g, 1 - t if v == 1 else t, 0 if v < 2 else u.count(1, -1 - KX * g))
                    sp.dma_start(sin[:, u.slot, t].rearrange("p e c -> p (e c)"), row) \
                        .then_inc(sin_in[u.slot], DMA)

            def store_s2(u):
                g = group_of(u.first)
                v = u.first - KX * g
                sp.wait_ge(sout_done, u.count(2, 2))
                for t in range(2):
                    if v < 2:
                        dst = rows_of(s2, g, v, 0)[:, t * GC:(t + 1) * GC]
                        src = sout[:, u.slot, 0, t]
                    else:
                        dst = rows_of(s2, g, t, u.count(1, -1 - KX * g))
                        src = sout[:, u.slot, t].rearrange("p e c -> p (e c)")
                    sp.dma_start(dst, src).then_inc(s2_put[u.slot], DMA)

            def spectral_unit(u):
                if u.first + 2 < UNITS:
                    sp.wait_ge(sin_lo_done, u.count(4, 4))
                    if u.first + 2 == KX:
                        for s in range(2):
                            sp.wait_ge(s1_put[s], 2 * DMA * ROWS // 2)
                    load_sin(u + 2)
                if 3 <= u.first < UNITS + 3:
                    store_s2(u + -3)

            def load_inverse(j):
                if j.first >= 2:
                    sp.wait_ge(inv_mm, j.count(4, -4))
                for t in range(2):
                    sp.dma_start(wmov[64 * t:64 * t + 64, j.slot].rearrange("p o e c -> p o (e c)"),
                                 packed_rows(s2, j.first // HALF, t, h_of(j))).then_inc(wsp_in[j.slot], DMA)
                if j.first >= 2:
                    sp.wait_ge(inv_out, j.count(4, -4))
                load_x(j, xr_in)

            def store_y(j):
                sp.wait_ge(inv_out, j.count(4, 4))
                for hh in range(2):
                    sp.dma_start(image(out, j.first // HALF, h_of(j), hh), wout[:, j.slot, hh]) \
                        .then_inc(y_put[j.slot], DMA)

            def inv_unit(j):
                if j.first + 1 < ROWS:
                    load_inverse(j + 1)
                if j.first >= 1:
                    store_y(j + -1)

            sp.dma_start(fw[:, :, :], fwd_w).then_inc(wconst_in, DMA)
            load_x(Index(0), x_in)
            load_x(Index(1), x_in)
            sp.dma_start(iw[:, :, :], inv_w).then_inc(wconst_in, DMA)
            for n, (w, b) in enumerate(((w1, b1), (w2, b2))):
                sp.dma_start(raw_m[0:BLOCK, n].rearrange("p (k o) -> p k o", k=8),
                             w.rearrange("k i o t -> i k (o t)")).then_inc(mlp_in, DMA)
                sp.dma_start(raw_m[BLOCK:BLOCK + 1, n], b.rearrange("(z k) o t -> z (k o t)", z=1)) \
                    .then_inc(mlp_in, DMA)
            sp.dma_start(raw_h[:, 0], fwd_h).then_inc(hconst_in, DMA)
            sp.dma_start(raw_h[:, 1], inv_h).then_inc(hconst_in, DMA)

            for k in range(2):
                fwd_unit(Index(k))
            with sp.Fori(0, (HALF - 4) // 2) as r:
                for k in range(2, 4):
                    fwd_unit(Index(k, r))
            for k in range(HALF - 2, HALF + LEAD):
                fwd_unit(Index(k))
            for s in range(2):
                sp.wait_ge(s1_put[s], 2 * DMA * HALF // 2)
            sp.wait_ge(prepared, PREPARED)
            load_sin(Index(0))
            load_sin(Index(1))
            for u in range(6):
                spectral_unit(Index(u))
                fwd_unit(Index(u + HALF + LEAD))
            with sp.Fori(0, 57) as r:
                for u in range(6, 8):
                    spectral_unit(Index(u, r))
                    fwd_unit(Index(u + HALF + LEAD, r))
            for u in range(120, INV_AT):
                if u + HALF + LEAD < ROWS:
                    spectral_unit(Index(u))
                    fwd_unit(Index(u + HALF + LEAD))
                else:
                    if u + HALF + LEAD == ROWS:
                        store_s1(Index(ROWS - 1))
                    spectral_unit(Index(u))
                if u == INV_AT - 1:
                    sp.wait_ge(s2_put[0], 2 * DMA * (KX // 2 + 1))
                    sp.wait_ge(s2_put[1], 2 * DMA * (KX // 2))
                    load_inverse(Index(0))
            for u in range(INV_AT, INV_AT + 2):
                spectral_unit(Index(u))
                inv_unit(Index(u - INV_AT))
            with sp.Fori(0, 60) as r:
                for u in range(INV_AT + 2, INV_AT + 4):
                    spectral_unit(Index(u, r))
                    inv_unit(Index(u - INV_AT, r))
            for u in range(INV_AT + 122, UNITS + 2):
                spectral_unit(Index(u))
                if u == UNITS + 1:
                    store_s2(Index(UNITS - 1))
                inv_unit(Index(u - INV_AT))
            rest = UNITS + 2 - INV_AT
            assert rest == HALF - 1
            for s in range(2):
                sp.wait_ge(s2_put[s], 2 * DMA * (UNITS // 2))
            for j in range(rest, HALF + 2):
                inv_unit(Index(j))
            with sp.Fori(0, (HALF - 4) // 2) as r:
                for j in range(HALF + 2, HALF + 4):
                    inv_unit(Index(j, r))
            for j in range(ROWS - 2, ROWS):
                inv_unit(Index(j))
            store_y(Index(ROWS - 1))
            for s in range(2):
                sp.wait_ge(y_put[s], 2 * DMA * ROWS // 2)

        @block.tensor
        def _(pe):
            def three_passes(bank, hi, lo, const_hi, const_lo, first, last, moving=False):
                pairs = ((hi, const_hi), (hi, const_lo), (lo, const_hi))
                for n, (data, const) in enumerate(pairs):
                    a, b = (const, data) if moving else (data, const)
                    mm = nc.tensor.matmul(bank, a, b, start=first and n == 0, stop=last and n == 2)
                return mm

            def forward_h(u, b):
                n = 4 * u.first + b
                if b == 0:
                    pe.wait_ge(sin_lo_done, u.count(4, 4))
                if n >= 2:
                    pe.wait_ge(spec_lo_done, u.count(4, b - 1))
                real_only = u.first - KX * group_of(u.first) < 2
                cols = slice(b * BLOCK, (b + 1) * BLOCK)
                for e in range(2):
                    bank = h_bank[b % 2][0:BLOCK, :].rearrange("p (t y) -> p t y", t=2)[:, :, e * 128:e * 128 + 128]
                    for t in range(1 if real_only else 2):
                        rows = slice(1, 3) if t == 0 else slice(0, 2)
                        mm = three_passes(bank, sin_hi[:, u.slot, t, e, cols], sin_lo[:, u.slot, t, e, cols],
                                          fh[:, 0, e, rows], fh[:, 1, e, rows],
                                          first=t == 0, last=real_only or t == 1)
                mm.then_inc(h_mm, 1)

            def layer1(u, b):
                i = 4 * u.first + b - 1
                blk, s = BLOCKS * group_of(i // 4) + i % 4, i % 2
                pe.wait_ge(spec_lo_done, u.count(4, b))
                if i >= 1:
                    pe.wait_ge(hid_lo_done, u.count(4, b - 1))
                both = l1_bank[0:BLOCK, :]
                three = ((spec_hi, 0, 1), (spec_hi, 1, 1), (spec_lo, 0, 0))
                for k, (data, part, bias) in enumerate(three):
                    rows = BLOCK + bias
                    if k < 2:
                        nc.tensor.matmul(both, m1[0:BLOCK, part, blk, 0], data[0:BLOCK, s], start=k == 0, stop=False)
                    nc.tensor.matmul(both[:, 0:SIDE], m1[0:rows, part, blk, 1], data[0:rows, s, 1],
                                     start=False, stop=False)
                    nc.tensor.matmul(both[:, SIDE:], m1[0:rows, part, blk, 2], data[0:rows, s, 0],
                                     start=False, stop=False)
                mm = nc.tensor.matmul(both, m1[0:BLOCK, 0, blk, 0], spec_lo[0:BLOCK, s], start=False, stop=True)
                mm.then_inc(l1_mm, 1)

            def layer2(u, b):
                i = 4 * u.first + b - 2
                blk, s = BLOCKS * group_of(i // 4) + i % 4, i % 2
                pe.wait_ge(hid_lo_done, u.count(4, b - 1))
                if i >= 1:
                    pe.wait_ge(shrunk_done, u.count(4, b - 2))
                for e in range(2):
                    bank = l2_bank[:, e * 192:e * 192 + 192]
                    ky = slice(e * 128, e * 128 + 128)
                    for k, (data, part, bias) in enumerate(((hid_hi, 0, 1), (hid_hi, 1, 1), (hid_lo, 0, 0))):
                        rows = BLOCK + bias
                        nc.tensor.matmul(bank, data[0:rows, s, 0, ky], m2[0:rows, part, blk, 1:3],
                                         start=k == 0, stop=False)
                        mm = nc.tensor.matmul(bank, data[0:BLOCK, s, 1, ky], m2[0:BLOCK, part, blk, 0:2],
                                              start=False, stop=k == 2)
                mm.then_inc(l2_mm, 1)

            def inverse_h(u, b):
                tile = (b + 1) % 4
                v = u + (-1 if b == 3 else -2)
                odd, im = tile % 2, tile // 2
                if tile == 0:
                    pe.wait_ge(shr_lo_done, v.count(4, 4))
                if v.first >= 1 or im:
                    pe.wait_ge(sout_done if odd else evens_done, v.count(2, im))
                bank = ih_bank[odd][:, 0:GC]
                for t in range(2):
                    c = (0, 2)[t] if im == 0 else (1, 0)[t]
                    mm = three_passes(bank, shr_hi[:, v.slot, odd, :, t], shr_lo[:, v.slot, odd, :, t],
                                      ih[:, 0, odd, c], ih[:, 1, odd, c], first=t == 0, last=t == 1, moving=True)
                mm.then_inc(iho_mm if odd else ihe_mm, 1)

            def spectral_step(u, b):
                n = 4 * u.first + b
                if n < STEPS:
                    forward_h(u, b)
                if 1 <= n < STEPS + 1:
                    layer1(u, b)
                if 7 <= n < STEPS + 7:
                    inverse_h(u, b)

            def layer2_step(u, b):
                if 2 <= 4 * u.first + b < STEPS + 2:
                    layer2(u, b)

            def fwd_tile(k, b):
                if b == 0:
                    pe.wait_ge(folded, k.count(2, 2))
                if 4 * k.first + b >= 2:
                    pe.wait_ge(fwd_out, k.count(4, b - 1))
                nc.tensor.matmul(w_bank[b % 2][:, 0:GC], fw[:, b // 2], wmov[:, k.slot, b // 2, b % 2],
                                 start=True, stop=True).then_inc(fwd_mm, 1)

            def inv_tile(j, b):
                if b == 0:
                    pe.wait_ge(wsp_in[j.slot], j.uses(1))
                if 4 * j.first + b >= 2:
                    pe.wait_ge(inv_out, j.count(4, b - 1))
                nc.tensor.matmul(w_bank[b % 2][:, 0:GC], iw[:, b % 2], wmov[:, j.slot, b % 2, b // 2],
                                 start=True, stop=True).then_inc(inv_mm, 1)

            def unit(u=None, fwd=None, inv=None):
                for b in range(4):
                    if u:
                        spectral_step(u, b)
                    if fwd:
                        fwd_tile(fwd, b)
                    if inv:
                        inv_tile(inv, b)
                    if u:
                        layer2_step(u, b)

            pe.wait_ge(wconst_in, 2 * DMA)
            for k in range(2):
                unit(fwd=Index(k))
            with pe.Fori(0, (HALF - 4) // 2) as r:
                for k in range(2, 4):
                    unit(fwd=Index(k, r))
            for k in range(HALF - 2, HALF + LEAD):
                unit(fwd=Index(k))
            pe.wait_ge(prepared, PREPARED)
            for u in range(6):
                unit(Index(u), fwd=Index(u + HALF + LEAD))
            with pe.Fori(0, 57) as r:
                for u in range(6, 8):
                    unit(Index(u, r), fwd=Index(u + HALF + LEAD, r))
            for u in range(120, INV_AT):
                unit(Index(u), fwd=Index(u + HALF + LEAD) if u + HALF + LEAD < ROWS else None)
            pe.wait_ge(fwd_out, 4 * ROWS)
            for u in range(INV_AT, INV_AT + 2):
                unit(Index(u), inv=Index(u - INV_AT))
            with pe.Fori(0, 60) as r:
                for u in range(INV_AT + 2, INV_AT + 4):
                    unit(Index(u, r), inv=Index(u - INV_AT, r))
            for u in range(INV_AT + 122, UNITS + 2):
                unit(Index(u), inv=Index(u - INV_AT))
            for j in range(HALF - 1, HALF + 2):
                unit(inv=Index(j))
            with pe.Fori(0, (HALF - 4) // 2) as r:
                for j in range(HALF + 2, HALF + 4):
                    unit(inv=Index(j, r))
            for j in range(ROWS - 2, ROWS):
                unit(inv=Index(j))

        @block.scalar
        def _(act):
            def spectral_step(u, b):
                n = 4 * u.first + b
                if 3 <= n < STEPS + 3:
                    act.wait_ge(l2_mm, u.count(4, b - 2))
                    if n >= 5:
                        act.wait_ge(shrunk_done, u.count(4, b - 4))
                    nc.scalar.activation(above[:, (n - 3) % 2].rearrange("p e t c -> p (e t c)"),
                                         l2_bank[:, 0:384], ACT.Relu, bias=minus2l[:, 0:1]).then_inc(above_done, 1)
                if n < STEPS:
                    act.wait_ge(h_mm, u.count(4, b + 1))
                    if n >= 2:
                        act.wait_ge(l1_mm, u.count(4, b - 1))
                    nc.scalar.activation(spec_hi[0:BLOCK, n % 2].rearrange("p t y -> p (t y)"),
                                         h_bank[b % 2][0:BLOCK, :], ACT.Copy).then_inc(spec_hi_done, 1)
                if 8 <= n < STEPS + 8 and b % 2 == 0:
                    im = b // 2
                    act.wait_ge(ihe_mm, u.count(2, im - 3))
                    if n >= 16:
                        act.wait_ge(sout_done, u.count(2, im - 5))
                    nc.scalar.activation(evens[:, im], ih_bank[0][:, 0:GC], ACT.Copy).then_inc(evens_done, 1)
                if 3 <= n < STEPS + 3:
                    act.wait_ge(shrunk_done, u.count(4, b - 2))
                    v, blk = (u, 0) if b == 3 else (u + -1, b + 1)
                    if blk == 0 and u.first >= 2:
                        act.wait_ge(iho_mm, u.count(2, -2))
                    nc.scalar.activation(shr_hi[:, v.slot, :, blk].rearrange("p e t c -> p e (t c)"),
                                         shrunk[:, (n - 3) % 2].rearrange("p e t c -> p e (t c)"),
                                         ACT.Copy).then_inc(shr_hi_done, 1)
                if 1 <= n < STEPS + 1:
                    act.wait_ge(l1_mm, u.count(4, b))
                    if n >= 3:
                        act.wait_ge(l2_mm, u.count(4, b - 2))
                    nc.scalar.activation(hid_hi[0:BLOCK, (n - 1) % 2].rearrange("p t y -> p (t y)"),
                                         l1_bank[0:BLOCK, :], ACT.Relu).then_inc(hid_hi_done, 1)
                if u.first + 1 < UNITS:
                    split_sin(u + 1, b)

            def split_sin(u, b):
                if b == 0:
                    act.wait_ge(sin_in[u.slot], u.uses(1))
                    if u.first >= 2:
                        act.wait_ge(h_mm, u.count(4, -4))
                nc.scalar.activation(sin_hi[:, u.slot, b // 2, b % 2], sin[:, u.slot, b // 2, b % 2],
                                     ACT.Copy).then_inc(sin_hi_done, 1)

            def fwd_out_tile(k, b):
                act.wait_ge(fwd_mm, k.count(4, b + 1))
                if b == 0 and k.first >= 2:
                    act.wait_ge(s1_put[k.slot], k.uses(0))
                nc.scalar.activation(wout[:, k.slot, b // 2, b % 2], w_bank[b % 2][:, 0:GC],
                                     ACT.Copy).then_inc(fwd_out, 1)

            def unit(u=None, fwd=None):
                for b in range(4):
                    if fwd and 4 * fwd.first + b >= 1:
                        fwd_out_tile(fwd if b else fwd + -1, (b - 1) % 4)
                    if u:
                        spectral_step(u, b)

            for k in range(2):
                unit(fwd=Index(k))
            with act.Fori(0, (HALF - 4) // 2) as r:
                for k in range(2, 4):
                    unit(fwd=Index(k, r))
            for k in range(HALF - 2, HALF + LEAD):
                unit(fwd=Index(k))
            act.wait_ge(prepared, PREPARED)
            for b in range(4):
                split_sin(Index(0), b)
            for u in range(6):
                unit(Index(u), fwd=Index(u + HALF + LEAD))
            with act.Fori(0, 57) as r:
                for u in range(6, 8):
                    unit(Index(u, r), fwd=Index(u + HALF + LEAD, r))
            for u in range(120, INV_AT):
                if u + HALF + LEAD == ROWS:
                    fwd_out_tile(Index(ROWS - 1), 3)
                unit(Index(u), fwd=Index(u + HALF + LEAD) if u + HALF + LEAD < ROWS else None)
            for u in range(INV_AT, INV_AT + 2):
                unit(Index(u))
            with act.Fori(0, 60) as r:
                for u in range(INV_AT + 2, INV_AT + 4):
                    unit(Index(u, r))
            for u in range(INV_AT + 122, UNITS + 2):
                unit(Index(u))

        @block.vector
        def _(dve):
            steps = [0]

            def prep(instruction):
                steps[0] += 1
                instruction.then_inc(prepared, 1)
                dve.wait_ge(prepared, steps[0])

            def prepare():
                nc.vector.memset(minus2l[:, :], -2.0 * LAMBDA).then_inc(prepared, 1)
                nc.vector.memset(spec_hi[BLOCK:BLOCK + 1, :, :, :].bitcast(F32), 1.0).then_inc(prepared, 1)
                nc.vector.memset(hid_hi[BLOCK:BLOCK + 1, :, :, :].bitcast(F32), 1.0).then_inc(prepared, 1)
                steps[0] = 3
                dve.wait_ge(hconst_in, 2 * DMA)
                for n, mat in enumerate((fh, ih)):
                    prep(nc.vector.tensor_copy(mat[:, :, :, :, :].rearrange("p a b c d -> p (a b c d)"), raw_h[:, n]))
                dve.wait_ge(mlp_in, 4 * DMA)
                prep(nc.vector.tensor_scalar(raw_m[BLOCK:BLOCK + 1, 1], raw_m[BLOCK:BLOCK + 1, 1],
                                             LAMBDA, None, ALU.add))
                for n, (mat, order) in enumerate(((m1, (0, 1, 2)), (m2, (1, 0, 2)))):
                    re_at, neg_at, im_at = order
                    raw = raw_m[:, n].rearrange("p (k o t) -> p k o t", k=8, t=2)
                    top, bias = slice(0, BLOCK), slice(BLOCK, BLOCK + 1)
                    parts = [(top, re_at, 0), (top, im_at, 1)]
                    parts += [(bias, 1, 0), (bias, 2, 1)]
                    for rows, at, t in parts:
                        prep(nc.vector.tensor_copy(mat[rows, 0, :, at], raw[rows, :, :, t]))
                        prep(nc.vector.tensor_tensor(mat[rows, 1, :, at], raw[rows, :, :, t],
                                                     mat[rows, 0, :, at].bitcast(F32), ALU.subtract))
                    for part in range(2):
                        prep(nc.vector.tensor_scalar(mat[top, part, :, neg_at], mat[top, part, :, im_at].bitcast(F32),
                                                     -1.0, None, ALU.mult))
                assert steps[0] == PREPARED

            def spectral_step(u, b):
                n = 4 * u.first + b
                if 3 <= n < STEPS + 3:
                    s = (n - 3) % 2
                    dve.wait_ge(above_done, u.count(4, b - 2))
                    if n >= 5:
                        dve.wait_ge(shr_lo_done, u.count(4, b - 4))
                    nc.vector.scalar_tensor_tensor(shrunk[:, s].rearrange("p e t c -> p (e t c)"), l2_bank[:, 0:384],
                                                   0.0, above[:, s].rearrange("p e t c -> p (e t c)"),
                                                   ALU.min, ALU.add).then_inc(shrunk_done, 1)
                if n < STEPS:
                    dve.wait_ge(spec_hi_done, u.count(4, b + 1))
                    nc.vector.tensor_tensor(spec_lo[:, n % 2].rearrange("p t y -> p (t y)"), h_bank[b % 2][0:BLOCK, :],
                                            spec_hi[0:BLOCK, n % 2].rearrange("p t y -> p (t y)").bitcast(F32),
                                            ALU.subtract).then_inc(spec_lo_done, 1)
                if 9 <= n < STEPS + 8 and b % 2 == 1:
                    im, v = b // 2, u + -2
                    dve.wait_ge(iho_mm, v.count(2, im + 1))
                    dve.wait_ge(evens_done, v.count(2, im + 1))
                    if im == 0 and v.first >= 2:
                        dve.wait_ge(s2_put[v.slot], v.uses(0))
                    nc.vector.tensor_tensor(sout[:, v.slot, im, 0], ih_bank[1][:, 0:GC], evens[:, im], ALU.add)
                    nc.vector.tensor_tensor(sout[:, v.slot, im, 1], evens[:, im], ih_bank[1][:, 0:GC],
                                            ALU.subtract).then_inc(sout_done, 1)
                if 3 <= n < STEPS + 3:
                    s = (n - 3) % 2
                    dve.wait_ge(shr_hi_done, u.count(4, b - 2))
                    v, blk = (u, 0) if b == 3 else (u + -1, b + 1)
                    nc.vector.tensor_tensor(shr_lo[:, v.slot, :, blk].rearrange("p e t c -> p e (t c)"),
                                            shrunk[:, s].rearrange("p e t c -> p e (t c)"),
                                            shr_hi[:, v.slot, :, blk].rearrange("p e t c -> p e (t c)").bitcast(F32),
                                            ALU.subtract).then_inc(shr_lo_done, 1)
                if u.first + 1 < UNITS:
                    split_sin(u + 1, b)
                if 1 <= n < STEPS + 1:
                    s = (n - 1) % 2
                    dve.wait_ge(hid_hi_done, u.count(4, b))
                    nc.vector.scalar_tensor_tensor(hid_lo[:, s].rearrange("p t y -> p (t y)"), l1_bank[0:BLOCK, :], 0.0,
                                                   hid_hi[0:BLOCK, s].rearrange("p t y -> p (t y)").bitcast(F32),
                                                   ALU.max, ALU.subtract).then_inc(hid_lo_done, 1)

            def split_sin(u, b):
                dve.wait_ge(sin_hi_done, u.count(4, b + 1))
                nc.vector.tensor_tensor(sin_lo[:, u.slot, b // 2, b % 2], sin[:, u.slot, b // 2, b % 2],
                                        sin_hi[:, u.slot, b // 2, b % 2].bitcast(F32),
                                        ALU.subtract).then_inc(sin_lo_done, 1)

            def fold(k, part):
                if part == 0:
                    dve.wait_ge(x_in[k.slot], k.uses(1))
                    if k.first >= 1:
                        dve.wait_ge(folded, k.count(2, 0))
                    nc.vector.tensor_tensor(hfold[:, 1], xt[:, k.slot, 0], xt[:, k.slot, 1],
                                            ALU.subtract).then_inc(hdif_done, 1)
                else:
                    if part == 1:
                        dve.wait_ge(hsum_done, k.count(1, 1))
                        dve.wait_ge(hdif_done, k.count(1, 1))
                        if k.first >= 2:
                            dve.wait_ge(fwd_mm, k.count(4, -4))
                    nc.vector.tensor_tensor(wmov[:, k.slot, part - 1], hfold[:, :, 0], hfold[:, :, 1],
                                            ALU.add if part == 1 else ALU.subtract).then_inc(folded, 1)

            def inv_out_tile(j, b):
                hh = b // 2
                dve.wait_ge(inv_mm, j.count(4, b + 1))
                if b == 0:
                    dve.wait_ge(xr_in[j.slot], j.uses(1))
                    if j.first >= 2:
                        dve.wait_ge(y_put[j.slot], j.uses(0))
                if b % 2:
                    dve.wait_ge(inv_out, j.count(4, b))
                bank = w_bank[b % 2][:, 0:GC]
                for v in range(2):
                    base = wout if b % 2 else xt
                    last = nc.vector.tensor_tensor(wout[:, j.slot, hh, v], base[:, j.slot, hh, v], bank,
                                                   ALU.subtract if b % 2 and v else ALU.add)
                last.then_inc(inv_out, 1)

            def unit(u=None, fwd=None, inv=None):
                for b in range(4):
                    if inv and 4 * inv.first + b >= 1:
                        inv_out_tile(inv if b else inv + -1, (b - 1) % 4)
                    if fwd and b < 3 and fwd.first + 1 < ROWS:
                        fold(fwd + 1, b)
                    if u:
                        spectral_step(u, b)

            for part in range(3):
                fold(Index(0), part)
            prepare()
            for k in range(2):
                unit(fwd=Index(k))
            with dve.Fori(0, (HALF - 4) // 2) as r:
                for k in range(2, 4):
                    unit(fwd=Index(k, r))
            for k in range(HALF - 2, HALF + LEAD):
                unit(fwd=Index(k))
            for b in range(4):
                split_sin(Index(0), b)
            for u in range(6):
                unit(Index(u), fwd=Index(u + HALF + LEAD))
            with dve.Fori(0, 57) as r:
                for u in range(6, 8):
                    unit(Index(u, r), fwd=Index(u + HALF + LEAD, r))
            for u in range(120, INV_AT):
                unit(Index(u), fwd=Index(u + HALF + LEAD) if u + HALF + LEAD < ROWS else None)
            for u in range(INV_AT, INV_AT + 2):
                unit(Index(u), inv=Index(u - INV_AT))
            with dve.Fori(0, 60) as r:
                for u in range(INV_AT + 2, INV_AT + 4):
                    unit(Index(u, r), inv=Index(u - INV_AT, r))
            for u in range(INV_AT + 122, UNITS + 2):
                unit(Index(u), inv=Index(u - INV_AT))
            for j in range(HALF - 1, HALF + 2):
                unit(inv=Index(j))
            with dve.Fori(0, (HALF - 4) // 2) as r:
                for j in range(HALF + 2, HALF + 4):
                    unit(inv=Index(j, r))
            for j in range(ROWS - 2, ROWS):
                unit(inv=Index(j))
            inv_out_tile(Index(ROWS - 1), 3)

        @block.gpsimd
        def _(pool):
            def hsum(k):
                pool.wait_ge(x_in[k.slot], k.uses(1))
                if k.first >= 1:
                    pool.wait_ge(folded, k.count(2, 0))
                nc.gpsimd.tensor_tensor(hfold[:, 0], xt[:, k.slot, 0], xt[:, k.slot, 1],
                                        ALU.add).then_inc(hsum_done, 1)

            for k in range(2):
                hsum(Index(k))
            with pool.Fori(0, (ROWS - 2) // 2) as r:
                for k in range(2, 4):
                    hsum(Index(k, r))


PREPARED = 26


def dft_constants():
    def parts(a):
        def twelve(v):
            m, e = np.frexp(v)
            return np.ldexp(np.rint(m * 4096.0) / 4096.0, e)
        hi = twelve(a)
        return np.stack([hi, twelve(a - hi)]).astype(np.float32)

    i = np.arange(HALF)
    scale = 1.0 / np.sqrt(SIDE)
    fwd_w, inv_w = np.zeros((HALF, 2, 128)), np.zeros((128, 2, HALF))
    fwd_h, inv_h = np.zeros((HALF, 2, 3, HALF)), np.zeros((HALF, 2, 3, HALF))
    for parity in range(2):
        angle = 2 * np.pi * ((np.outer(i, 2 * i + parity)) % SIDE) / SIDE
        cos, sin = scale * np.cos(angle), scale * np.sin(angle)
        kx = 64
        fwd_w[:, parity, 0:kx], fwd_w[:, parity, kx:] = cos[:, 0:kx], -sin[:, 0:kx]
        inv_w[0:kx, parity], inv_w[kx:, parity] = 2 * cos[:, 0:kx].T, -2 * sin[:, 0:kx].T
        fwd_h[:, parity, 0], fwd_h[:, parity, 1], fwd_h[:, parity, 2] = sin, cos, -sin
        inv_h[:, parity, 0], inv_h[:, parity, 1], inv_h[:, parity, 2] = cos.T, sin.T, -sin.T
    nyquist = scale * (1.0 - 2.0 * (i % 2))
    fwd_w[:, 0, 64] = nyquist
    inv_w[0, 0], inv_w[64, 0] = scale, nyquist
    split = lambda a: np.ascontiguousarray(parts(a).transpose(1, 0, 2, 3, 4).reshape(HALF, -1))
    return fwd_w.astype(np.float32), inv_w.astype(np.float32), split(fwd_h), split(inv_h)


def kernel(**inputs):
    import concourse.bacc as bacc
    from concourse.bass_utils import run_bass_kernel_spmd

    nc = bacc.Bacc("TRN2", target_bir_lowering=False, num_devices=1)
    fwd_w, inv_w, fwd_h, inv_h = dft_constants()
    arrays = {name: np.ascontiguousarray(inputs[name]) for name in
              ("x", "L0_conv_w1", "L0_conv_b1", "L0_conv_w2", "L0_conv_b2")}
    arrays.update(fwd_w=fwd_w, inv_w=inv_w, fwd_h=fwd_h, inv_h=inv_h)
    args = [nc.dram_tensor("in_" + name, a.shape, mybir.dt.from_np(a.dtype), kind="ExternalInput").ap()
            for name, a in arrays.items()]
    out = nc.dram_tensor("out_dram", arrays["x"].shape, F32, kind="ExternalOutput").ap()
    spectral_conv(nc, *args, out)
    result = run_bass_kernel_spmd(nc, [{"in_" + name: a for name, a in arrays.items()}], core_ids=[0])
    return result.results[0]["out_dram"]
```

```python
from contextlib import ExitStack

import numpy as np

import concourse.bass as bass
from concourse import mybir

ALU = mybir.AluOpType
ACT = mybir.ActivationFunctionType
F32 = mybir.dt.float32
F32R = mybir.dt.float32r

LAMBDA = float(np.float32(0.01))
SIDE = 256
HALF = SIDE // 2
CHANNELS = 768
BLOCK = 96
NBLOCKS = CHANNELS // BLOCK
GROUPS = 4
GC = CHANNELS // GROUPS
PAIR = 2 * GC
KX = HALF + 1
UNITS = GROUPS * KX
STEPS = 2 * UNITS
QUAD = HALF // 2
WUNITS = GROUPS * QUAD
PITCH = HALF * PAIR + 1024
LEAD = 2
LAG = 6
DMA = 16
SPAN = 8
LOOP_FROM, LOOPS = 12, 13
SP_FROM, SP_LOOPS = 14, 13
ALONE = WUNITS - QUAD


class Index:

    def __init__(self, first, reg=None, stride=0):
        self.first, self.reg, self.stride, self.slot = first, reg, stride, first % 2

    def count(self, times=1, plus=0):
        value = times * self.first + plus
        return value if self.reg is None else self.reg * (times * self.stride) + value

    def uses(self, plus, dmas):
        value = dmas * DMA * (self.first // 2 + plus)
        return value if self.reg is None else self.reg * (dmas * DMA * self.stride // 2) + value

    def __add__(self, n):
        return Index(self.first + n, self.reg, self.stride)

    def __sub__(self, n):
        return self + -n


def group_of(unit):
    return unit // KX


def forward_at(g, u, b, reg):
    pos = 2 * u + b + 4 * LEAD
    if g < GROUPS - 1 and pos // 4 < QUAD + LEAD:
        return Index(QUAD * (g + 1) + pos // 4, reg, SPAN // 2), pos % 4
    return None, 0


def inverse_at(g, u, b, reg):
    pos = 2 * (u - LAG) + b
    if g >= 1 and pos >= 0:
        return Index(QUAD * (g - 1) + pos // 4, reg, SPAN // 2), pos % 4
    pos += 2 * KX
    if g >= 2 and pos < 4 * QUAD:
        return Index(QUAD * (g - 2) + pos // 4, reg, SPAN // 2), pos % 4
    return None, 0


def walk(engine, unit, loop_from=LOOP_FROM, loops=LOOPS):
    for g in range(GROUPS):
        last = KX if g < GROUPS - 1 else (4 * QUAD) // 2 + LAG
        for u in range(loop_from):
            unit(g, u, None)
        with engine.Fori(0, loops) as r:
            for u in range(loop_from, loop_from + SPAN):
                unit(g, u, r)
        for u in range(loop_from + SPAN * loops, last):
            unit(g, u, None)


def walk_w(engine, unit, first, start, end, last):
    for k in range(first, start):
        unit(Index(k))
    with engine.Fori(0, (end - start) // 2) as r:
        for k in range(start, start + 2):
            unit(Index(k, r, 2))
    for k in range(end, last):
        unit(Index(k))


def spectral_conv(nc, x, w1, b1, w2, b2, fwd_w, inv_w, fwd_h, inv_h, out):
    s1 = nc.dram_tensor("s1_scratch", (GROUPS, 2, HALF, PITCH), F32, kind="Internal").ap()
    s2 = nc.dram_tensor("s2_scratch", (GROUPS, 2, HALF, PITCH), F32, kind="Internal").ap()

    with ExitStack() as ctx:
        def sb(name, shape, dt=F32):
            return ctx.enter_context(nc.sbuf_tensor(name, shape, dt))

        def ps(name):
            return ctx.enter_context(nc.psum_tensor(name, [128, 512], F32))

        def sem(name):
            return ctx.enter_context(nc.semaphore(name))

        xt = sb("xt", [128, 2, 2, 2, 2, GC])
        hf = sb("hf", [128, 2, 2, 2, GC])
        pf = sb("pf", [128, 2, 2, 2, GC])
        wmov = sb("wmov", [128, 2, 2, 2, PAIR])
        wout = sb("wout", [128, 2, 2, 2, PAIR])
        vmov = sb("vmov", [128, 2, 2, 2, PAIR])
        xr = sb("xr", [128, 2, 2, 2, 2, GC])
        vev = sb("vev", [128, 2, PAIR])
        vw = sb("vw", [128, 2, 2, PAIR])
        vp = sb("vp", [128, 2, 2, 2, GC])
        yt = sb("yt", [128, 2, 2, 2, 2, GC])
        sin = sb("sin", [128, 2, 2, PAIR])
        sin_hi = sb("sin_hi", [128, 2, 2, PAIR], F32R)
        sin_lo = sb("sin_lo", [128, 2, 2, PAIR], F32R)
        spec_hi = sb("spec_hi", [BLOCK + 1, 2, 2, SIDE], F32R)
        spec_lo = sb("spec_lo", [BLOCK, 2, 2, SIDE], F32R)
        hid_hi = sb("hid_hi", [BLOCK + 1, 2, 2, SIDE], F32R)
        hid_lo = sb("hid_lo", [BLOCK, 2, 2, SIDE], F32R)
        above = sb("above", [128, 2, 2, 2 * BLOCK])
        shrunk = sb("shrunk", [128, 2, 2, 2 * BLOCK])
        shr_hi = sb("shr_hi", [128, 2, 2, 2, 2 * BLOCK], F32R)
        shr_lo = sb("shr_lo", [128, 2, 2, 2, 2 * BLOCK], F32R)
        sout = sb("sout", [128, 2, 2, 2, GC])
        fw = sb("fw", [128, 2, 128])
        iw = sb("iw", [128, 2, 2, 128])
        fh = sb("fh", [128, 2, 2, 4, 128], F32R)
        ih = sb("ih", [128, 2, 2, 128], F32R)
        m1 = sb("m1", [BLOCK + 1, 2, NBLOCKS, 3, BLOCK], F32R)
        m2 = sb("m2", [BLOCK + 1, 2, NBLOCKS, 3, BLOCK], F32R)
        minus2l = sb("minus2l", [128, 1])

        h_bank = [ps("h_bank0"), ps("h_bank1")]
        l1_bank, l2_bank = ps("l1_bank"), ps("l2_bank")
        ih_bank = [ps("ih_even"), ps("ih_odd")]
        fwd_beside, inv_beside = ps("fwd_bank"), ps("inv_bank")

        wconst_in, hconst_in, mlp_in = sem("wconst_in"), sem("hconst_in"), sem("mlp_in")
        prepared = sem("prepared")
        x_in = [sem("x_in0"), sem("x_in1")]
        hfold_done = [sem("hfold0_done"), sem("hfold1_done")]
        pfold_done = sem("pfold_done")
        wfold_done = sem("wfold_done")
        fwd_mm = sem("fwd_mm")
        fwd_out = sem("fwd_out")
        s1_put = [sem("s1_put0"), sem("s1_put1")]
        s1_edge = sem("s1_edge")
        sin_in = [sem("sin_in0"), sem("sin_in1")]
        sin_hi_done, sin_lo_done = sem("sin_hi_done"), sem("sin_lo_done")
        h_mm, l1_mm, l2_mm = sem("h_mm"), sem("l1_mm"), sem("l2_mm")
        spec_hi_done, spec_lo_done = sem("spec_hi_done"), sem("spec_lo_done")
        hid_hi_done, hid_lo_done = sem("hid_hi_done"), sem("hid_lo_done")
        above_done, shrunk_done = sem("above_done"), sem("shrunk_done")
        shr_hi_done, shr_lo_done = sem("shr_hi_done"), sem("shr_lo_done")
        ih_mm, ih_out = sem("ih_mm"), sem("ih_out")
        s2_put = [sem("s2_put0"), sem("s2_put1")]
        s2_edge = [sem("s2_edge0"), sem("s2_edge1")]
        v_in = [sem("v_in0"), sem("v_in1")]
        v_edge = sem("v_edge")
        xr_in = [sem("xr_in0"), sem("xr_in1")]
        inv_mm = sem("inv_mm")
        vev_done = sem("vev_done")
        vw_done = sem("vw_done")
        vp_done = sem("vp_done")
        yt_rows = sem("yt_rows")
        yt_done = sem("yt_done")
        y_put = [sem("y_put0"), sem("y_put1")]

        raw_h = yt[:, 0].rearrange("p a b v c -> p (a b v c)")
        raw_i = vw[:, :, :, :].rearrange("p a b c -> p (a b c)")
        raw_m = xr[:, :, :, :, :, :].rearrange("p s a b v c -> p s (a b v c)")

        def tile_of(scratch, g, t, q):
            return scratch[g, t, q, 0:HALF * PAIR].rearrange("(h c) -> h c", h=HALF)

        def slots_of(scratch, g, t, row):
            return scratch[g, t].rearrange("(o k) c -> k o c", o=2)[:, :, bass.ts(row, PAIR)]

        def local(k):
            return k.count(1, -QUAD * (k.first // QUAD))

        def mirrored(k):
            if k.first % QUAD == 0:
                return HALF // 2
            value = HALF - k.first % QUAD
            return value if k.reg is None else k.reg * -k.stride + value

        def fwd_bank(k, tile):
            return fwd_beside if k.first >= QUAD + LEAD else [fwd_beside, inv_beside, *h_bank][tile]

        def inv_bank(j, tile):
            if j.first < ALONE:
                return inv_beside
            return [[inv_beside, fwd_beside, *h_bank], [l1_bank, l2_bank, *ih_bank]][j.slot][tile]

        def vw_of(j):
            if j.first >= ALONE and j.slot:
                return [part[:, :, :, :].rearrange("p v e c -> p (v e c)") for part in (above, shrunk)]
            return [vw[:, form].rearrange("p v c -> p (v c)") for form in range(2)]

        def vp_of(j):
            return sout[:, :, :, :, :] if j.first >= ALONE and j.slot else vp[:, :, :, :, :]

        def store_y(queue, j):
            queue.wait_ge(yt_done, j.count(1, 1))
            for pair in range(2):
                for hh in range(2):
                    queue.dma_start(image(out, j, pair, hh), yt[:, j.slot, pair, hh]).then_inc(y_put[j.slot], DMA)

        def image(a, k, pair, hh):
            g = k.first // QUAD
            row = a[0, HALF * hh:HALF * (hh + 1)][mirrored(k) if pair else local(k)]
            return row.rearrange("(v w) c -> w v c", v=2)[:, :, g * GC:(g + 1) * GC]

        block = ctx.enter_context(nc.Block())

        @block.sync
        def _(sp):
            def load_rows(tile, k, landed):
                for pair in range(2):
                    for hh in range(2):
                        sp.dma_start(tile[:, k.slot, pair, hh], image(x, k, pair, hh)).then_inc(landed[k.slot], DMA)

            def store_s1(k):
                sp.wait_ge(fwd_out, k.count(4, 4))
                g = k.first // QUAD
                for t in range(2):
                    part = slice(64 * t, 64 * t + 64)
                    sp.dma_start(slots_of(s1, g, t, local(k)), wout[part, k.slot, :, 0]) \
                        .then_inc(s1_put[k.slot], DMA)
                    if k.first % QUAD:
                        sp.dma_start(slots_of(s1, g, 1 - t, local(k) + QUAD), wout[part, k.slot, :, 1]) \
                            .then_inc(s1_put[k.slot], DMA)
                    else:
                        sp.dma_start(slots_of(s1, g, t, QUAD)[:, :, 0:GC], wout[part, k.slot, :, 1, 0:GC]) \
                            .then_inc(s1_put[k.slot], DMA)
                        sp.dma_start(slots_of(s1, g, 1 - t, QUAD)[:, :, GC:], wout[part, k.slot, :, 1, GC:]) \
                            .then_inc(s1_edge, DMA)

            def fwd_unit(k):
                if k.first + 3 < WUNITS:
                    for pair in range(2):
                        sp.wait_ge(hfold_done[pair], k.count(1, 2))
                    load_rows(xt, k + 3, x_in)
                if 1 <= k.first < WUNITS + 1:
                    store_s1(k - 1)

            def load_sin(u):
                g = group_of(u.first)
                v = u.first - KX * g
                if v == 0:
                    for s in range(2):
                        sp.wait_ge(s1_put[s], 4 * DMA * QUAD // 2 * (g + 1))
                    sp.wait_ge(s1_edge, 2 * DMA * (g + 1))
                for t in range(2):
                    sp.dma_start(sin[:, u.slot, t], tile_of(s1, g, t, 0 if v < 2 else u.count(1, -1 - KX * g))) \
                        .then_inc(sin_in[u.slot], DMA)

            def store_s2(u):
                g = group_of(u.first)
                v = u.first - KX * g
                sp.wait_ge(ih_out, u.count(2, 2))
                if v >= 2:
                    for t in range(2):
                        sp.dma_start(tile_of(s2, g, t, u.count(1, -1 - KX * g)),
                                     sout[:, u.slot, t].rearrange("p e c -> p (e c)")).then_inc(s2_put[u.slot], DMA)
                    return
                re_at, im_at = tile_of(s2, g, v, 0), tile_of(s2, g, 1 - v, 0)
                sp.dma_start(re_at[0:64], sout[0:64, u.slot, 0].rearrange("p e c -> p (e c)")) \
                    .then_inc(s2_put[u.slot], DMA)
                sp.dma_start(im_at[65:128], sout[65:128, u.slot, 1].rearrange("p e c -> p (e c)")) \
                    .then_inc(s2_put[u.slot], DMA)
                sp.dma_start(re_at[64:65, 0:GC], sout[64:65, u.slot, 0, 0]).then_inc(s2_edge[u.slot], DMA)
                sp.dma_start(im_at[64:65, GC:], sout[64:65, u.slot, 1, 1]).then_inc(s2_edge[u.slot], DMA)

            def load_vmov(j):
                g = j.first // QUAD
                if j.first % QUAD == 0:
                    for s in range(2):
                        sp.wait_ge(s2_put[s], 2 * DMA * ((KX * (g + 1) + 1 - s) // 2))
                        sp.wait_ge(s2_edge[s], 2 * DMA * (g + 1))
                if j.first >= 2:
                    sp.wait_ge(inv_mm, j.count(4, -4))
                for t in (1, 0):
                    part = slice(64 * t, 64 * t + 64)
                    sp.dma_start(vmov[part, j.slot, 0], slots_of(s2, g, t, local(j))).then_inc(v_in[j.slot], DMA)
                    if j.first % QUAD:
                        sp.dma_start(vmov[part, j.slot, 1], slots_of(s2, g, 1 - t, local(j) + QUAD)) \
                            .then_inc(v_in[j.slot], DMA)
                    else:
                        sp.dma_start(vmov[part, j.slot, 1, :, 0:GC], slots_of(s2, g, t, QUAD)[:, :, 0:GC]) \
                            .then_inc(v_in[j.slot], DMA)
                        sp.dma_start(vmov[part, j.slot, 1, :, GC:], slots_of(s2, g, 1 - t, QUAD)[:, :, GC:]) \
                            .then_inc(v_edge, DMA)

            def inv_unit(j):
                if (j.first + 1) % QUAD and j.first < WUNITS:
                    load_vmov(j + 1)
                if 1 <= j.first < WUNITS + 1:
                    if j.first >= 3:
                        sp.wait_ge(yt_done, j.count(1, -2))
                    load_rows(xr, j - 1, xr_in)
                if 3 <= j.first < ALONE:
                    store_y(sp, j - 3)

            def unit(g, u, reg):
                at = Index(KX * g + u, reg, SPAN)
                if at.first + 2 < UNITS:
                    sp.wait_ge(sin_lo_done, at.count(2, 2))
                    load_sin(at + 2)
                if 4 <= at.first < UNITS + 4:
                    store_s2(at - 4)
                for b in range(2):
                    k, tile = forward_at(g, u, b, reg)
                    if k and tile == 0:
                        fwd_unit(k)
                    j, tile = inverse_at(g, u, b, reg)
                    if j and tile == 0:
                        inv_unit(j)
                if u == LAG - 1 and g >= 1:
                    load_vmov(Index(QUAD * (g - 1)))

            sp.dma_start(fw[:, :, :], fwd_w).then_inc(wconst_in, DMA)
            for k in range(2):
                load_rows(xt, Index(k), x_in)
            for n, (w, b) in enumerate(((w1, b1), (w2, b2))):
                sp.dma_start(raw_m[0:BLOCK, n].rearrange("p (k o) -> p k o", k=NBLOCKS),
                             w.rearrange("k i o t -> i k (o t)")).then_inc(mlp_in, DMA)
                sp.dma_start(raw_m[BLOCK:BLOCK + 1, n], b.rearrange("(z k) o t -> z (k o t)", z=1)) \
                    .then_inc(mlp_in, DMA)
            for n in range(2):
                sp.dma_start(raw_h[:, 0:1024], fwd_h[:, n]).then_inc(hconst_in, DMA)
                sp.wait_ge(prepared, 4 + n)
            sp.dma_start(raw_i[:, 0:512], inv_h).then_inc(hconst_in, DMA)
            sp.dma_start(iw[:, :, :, :], inv_w).then_inc(wconst_in, DMA)
            for pair in range(2):
                sp.wait_ge(hfold_done[pair], 1)
            load_rows(xt, Index(2), x_in)

            walk_w(sp, fwd_unit, 0, 2, QUAD - 4, QUAD + LEAD)
            sp.wait_ge(prepared, PREPARED)
            load_sin(Index(0))
            load_sin(Index(1))
            walk(sp, unit, SP_FROM, SP_LOOPS)
            load_vmov(Index(ALONE))
            walk_w(sp, inv_unit, ALONE, ALONE + 2, WUNITS - 2, WUNITS + 1)
            for s in range(2):
                sp.wait_ge(y_put[s], 4 * DMA * WUNITS // 2)

        @block.tensor
        def _(pe):
            def forward_h(u, b):
                n = 2 * u.first + b
                if b == 0:
                    pe.wait_ge(sin_lo_done, u.count(2, 2))
                if n >= 2:
                    pe.wait_ge(spec_lo_done, u.count(2, b - 1))
                v = u.first - KX * group_of(u.first)
                plan = {0: ((0, 2), (1, 3)), 1: ((1, 2), (0, 3))}.get(v, ((0, 0), (1, 1)))
                for e in range(2):
                    cols = slice(e * GC + b * BLOCK, e * GC + (b + 1) * BLOCK)
                    for t, (tile, matrix) in enumerate(plan):
                        bank = h_bank[b][0:BLOCK, t * SIDE + e * HALF:t * SIDE + (e + 1) * HALF]
                        for p, (data, part) in enumerate(((sin_hi, 0), (sin_hi, 1), (sin_lo, 0))):
                            mm = nc.tensor.matmul(bank, data[:, u.slot, tile, cols], fh[:, part, e, matrix],
                                                  start=p == 0, stop=p == 2)
                mm.then_inc(h_mm, 1)

            def layer1(u, b):
                i = 2 * u.first + b - 1
                blk, s = 2 * group_of(i // 2) + i % 2, i % 2
                pe.wait_ge(spec_lo_done, u.count(2, b))
                if i >= 1:
                    pe.wait_ge(hid_lo_done, u.count(2, b - 1))
                both = l1_bank[0:BLOCK, :]
                for p, (data, part, bias) in enumerate(((spec_hi, 0, 1), (spec_hi, 1, 1), (spec_lo, 0, 0))):
                    rows = BLOCK + bias
                    if p < 2:
                        nc.tensor.matmul(both, m1[0:BLOCK, part, blk, 0], data[0:BLOCK, s], start=p == 0, stop=False)
                    nc.tensor.matmul(both[:, 0:SIDE], m1[0:rows, part, blk, 1], data[0:rows, s, 1],
                                     start=False, stop=False)
                    nc.tensor.matmul(both[:, SIDE:], m1[0:rows, part, blk, 2], data[0:rows, s, 0],
                                     start=False, stop=False)
                nc.tensor.matmul(both, m1[0:BLOCK, 0, blk, 0], spec_lo[0:BLOCK, s], start=False, stop=True) \
                    .then_inc(l1_mm, 1)

            def layer2(u, b):
                i = 2 * u.first + b - 2
                blk, s = 2 * group_of(i // 2) + i % 2, i % 2
                pe.wait_ge(hid_lo_done, u.count(2, b - 1))
                if i >= 1:
                    pe.wait_ge(shrunk_done, u.count(2, b - 2))
                for e in range(2):
                    bank = l2_bank[:, e * 2 * BLOCK:(e + 1) * 2 * BLOCK]
                    ky = slice(e * HALF, (e + 1) * HALF)
                    for p, (data, part, bias) in enumerate(((hid_hi, 0, 1), (hid_hi, 1, 1), (hid_lo, 0, 0))):
                        rows = BLOCK + bias
                        nc.tensor.matmul(bank, data[0:rows, s, 0, ky], m2[0:rows, part, blk, 1:3],
                                         start=p == 0, stop=False)
                        mm = nc.tensor.matmul(bank, data[0:BLOCK, s, 1, ky], m2[0:BLOCK, part, blk, 0:2],
                                              start=False, stop=p == 2)
                mm.then_inc(l2_mm, 1)

            def inverse_h(u, b):
                v, e = (u - 2, 0) if b else (u - 3, 1)
                if e == 0:
                    pe.wait_ge(shr_lo_done, v.count(2, 2))
                if v.first >= 1:
                    pe.wait_ge(ih_out, v.count(2, e - 1))
                for p, (part, data) in enumerate(((0, shr_hi), (1, shr_hi), (0, shr_lo))):
                    mm = nc.tensor.matmul(ih_bank[e][:, 0:PAIR], ih[:, part, e], data[:, v.slot, e],
                                          start=p == 0, stop=p == 2)
                mm.then_inc(ih_mm, 1)

            def fwd_tile(k, tile):
                if tile == 0:
                    pe.wait_ge(wfold_done, k.count(2, 2))
                if k.first >= QUAD + LEAD:
                    pe.wait_ge(fwd_out, k.count(4, tile))
                elif k.first >= 1:
                    pe.wait_ge(fwd_out, k.count(4, tile - 3))
                nc.tensor.matmul(fwd_bank(k, tile)[:, 0:PAIR], fw[:, tile // 2], wmov[:, k.slot, tile // 2, tile % 2],
                                 start=True, stop=True).then_inc(fwd_mm, 1)

            def inv_tile(j, tile):
                form, o = tile // 2, tile % 2
                bank = inv_bank(j, tile)
                if tile == 0:
                    pe.wait_ge(v_in[j.slot], j.uses(1, 4))
                if j.first >= ALONE:
                    if j.first >= ALONE + 2:
                        pe.wait_ge(vw_done if o else vev_done, j.count(2, form - 3))
                elif o:
                    pe.wait_ge(vev_done, j.count(2, form + 1))
                elif 2 * j.first + form >= 1:
                    pe.wait_ge(vw_done, j.count(2, form))
                if form and j.first % QUAD == 0:
                    if o == 0:
                        pe.wait_ge(v_edge, 2 * DMA * (j.first // QUAD + 1))
                    nc.tensor.matmul(bank[:, 0:GC], iw[:, 0, o], vmov[:, j.slot, 1, o, 0:GC],
                                     start=True, stop=True)
                    nc.tensor.matmul(bank[:, GC:PAIR], iw[:, 1, o], vmov[:, j.slot, 1, o, GC:],
                                     start=True, stop=True).then_inc(inv_mm, 1)
                else:
                    nc.tensor.matmul(bank[:, 0:PAIR], iw[:, form, o], vmov[:, j.slot, form, o],
                                     start=True, stop=True).then_inc(inv_mm, 1)

            def unit(g, u, reg):
                at = Index(KX * g + u, reg, SPAN)
                for b in range(2):
                    n = 2 * at.first + b
                    if n < STEPS:
                        forward_h(at, b)
                    if 1 <= n < STEPS + 1:
                        layer1(at, b)
                    if 5 <= n < STEPS + 5:
                        inverse_h(at, b)
                    k, tile = forward_at(g, u, b, reg)
                    if k and k.first < WUNITS:
                        fwd_tile(k, tile)
                    j, tile = inverse_at(g, u, b, reg)
                    if j:
                        inv_tile(j, tile)
                    if 2 <= n < STEPS + 2:
                        layer2(at, b)

            def fwd_alone(k):
                for tile in range(4):
                    fwd_tile(k, tile)

            def inv_alone(j):
                for tile in range(4):
                    inv_tile(j, tile)

            pe.wait_ge(wconst_in, 2 * DMA)
            walk_w(pe, fwd_alone, 0, 2, QUAD, QUAD + LEAD)
            pe.wait_ge(prepared, PREPARED)
            pe.wait_ge(fwd_out, 4 * (QUAD + LEAD))
            walk(pe, unit)
            pe.wait_ge(vw_done, 2 * ALONE)
            pe.wait_ge(fwd_out, 4 * WUNITS)
            pe.wait_ge(shrunk_done, STEPS)
            pe.wait_ge(ih_out, STEPS)
            walk_w(pe, inv_alone, ALONE, ALONE + 2, WUNITS, WUNITS)

        @block.scalar
        def _(act):
            def fwd_out_tile(k, tile):
                act.wait_ge(fwd_mm, k.count(4, tile + 1))
                if tile == 0 and k.first >= 2:
                    act.wait_ge(s1_put[k.slot], k.uses(0, 4))
                    if k.first % QUAD == 2:
                        act.wait_ge(s1_edge, 2 * DMA * (k.first // QUAD + 1))
                nc.scalar.activation(wout[:, k.slot, tile // 2, tile % 2], fwd_bank(k, tile)[:, 0:PAIR],
                                     ACT.Copy).then_inc(fwd_out, 1)

            def inv_even(j, form):
                act.wait_ge(inv_mm, j.count(4, 2 * form + 1))
                if j.first >= 1:
                    act.wait_ge(vw_done, j.count(2, form - 1))
                nc.scalar.activation(vev[:, form], inv_bank(j, 2 * form)[:, 0:PAIR], ACT.Copy).then_inc(vev_done, 1)

            def split_sin(u, t):
                if t == 0:
                    act.wait_ge(sin_in[u.slot], u.uses(1, 2))
                    if u.first >= 2:
                        act.wait_ge(h_mm, u.count(2, -2))
                nc.scalar.activation(sin_hi[:, u.slot, t], sin[:, u.slot, t], ACT.Copy).then_inc(sin_hi_done, 1)

            def step(u, b):
                n = 2 * u.first + b
                if 3 <= n < STEPS + 3:
                    act.wait_ge(l2_mm, u.count(2, b - 2))
                    if n >= 5:
                        act.wait_ge(shrunk_done, u.count(2, b - 4))
                    nc.scalar.activation(above[:, (n - 3) % 2].rearrange("p e c -> p (e c)"),
                                         l2_bank[:, 0:PAIR], ACT.Relu, bias=minus2l[:, 0:1]).then_inc(above_done, 1)
                if n < STEPS:
                    act.wait_ge(h_mm, u.count(2, b + 1))
                    if n >= 2:
                        act.wait_ge(l1_mm, u.count(2, b - 1))
                    nc.scalar.activation(spec_hi[0:BLOCK, n % 2].rearrange("p t y -> p (t y)"),
                                         h_bank[b][0:BLOCK, :], ACT.Copy).then_inc(spec_hi_done, 1)
                if 6 <= n < STEPS + 6:
                    v = u - 3
                    act.wait_ge(ih_mm, v.count(2, b + 1))
                    if b == 0 and v.first >= 2:
                        act.wait_ge(s2_put[v.slot], v.uses(0, 2))
                        g = group_of(v.first)
                        if 2 <= v.first - KX * g < 4:
                            act.wait_ge(s2_edge[v.slot], 2 * DMA * (g + 1))
                    nc.scalar.activation(sout[:, v.slot, :, b].rearrange("p t (k c) -> p k t c", k=2),
                                         ih_bank[b][:, 0:PAIR].rearrange("p (k t c) -> p k t c", k=2, t=2),
                                         ACT.Copy).then_inc(ih_out, 1)
                if 3 <= n < STEPS + 3:
                    act.wait_ge(shrunk_done, u.count(2, b - 2))
                    v, blk = (u - 1, 0) if b else (u - 2, 1)
                    if blk == 0 and v.first >= 2:
                        act.wait_ge(ih_mm, v.count(2, -2))
                    nc.scalar.activation(shr_hi[:, v.slot, :, blk], shrunk[:, (n - 3) % 2],
                                         ACT.Copy).then_inc(shr_hi_done, 1)
                if 1 <= n < STEPS + 1:
                    act.wait_ge(l1_mm, u.count(2, b))
                    if n >= 3:
                        act.wait_ge(l2_mm, u.count(2, b - 2))
                    nc.scalar.activation(hid_hi[0:BLOCK, (n - 1) % 2].rearrange("p t y -> p (t y)"),
                                         l1_bank[0:BLOCK, :], ACT.Relu).then_inc(hid_hi_done, 1)
                if u.first + 1 < UNITS:
                    split_sin(u + 1, b)

            def unit(g, u, reg):
                for b in range(2):
                    step(Index(KX * g + u, reg, SPAN), b)
                    k, tile = forward_at(g, u, b, reg)
                    if k and k.first < WUNITS:
                        fwd_out_tile(k, tile)
                    j, tile = inverse_at(g, u, b, reg)
                    if j and tile % 2 == 0:
                        inv_even(j, tile // 2)

            def fwd_alone(k):
                for tile in range(4):
                    fwd_out_tile(k, tile)

            def inv_alone(j):
                if j.first < WUNITS:
                    for form in range(2):
                        inv_even(j, form)
                store_y(act, j - 2)

            walk_w(act, fwd_alone, 0, 4, QUAD, QUAD + LEAD)
            act.wait_ge(prepared, PREPARED)
            for t in range(2):
                split_sin(Index(0), t)
            walk(act, unit)
            store_y(act, Index(ALONE - 3))
            walk_w(act, inv_alone, ALONE, ALONE + 4, WUNITS, WUNITS + 2)

        def fold_h(eng, vec, k, pair):
            eng.wait_ge(x_in[k.slot], k.uses(1, 4))
            if k.first >= 1:
                eng.wait_ge(pfold_done, k.count(1, 0))
            vec.tensor_tensor(hf[:, pair, 0], xt[:, k.slot, pair, 0], xt[:, k.slot, pair, 1], ALU.add)
            vec.tensor_tensor(hf[:, pair, 1], xt[:, k.slot, pair, 0], xt[:, k.slot, pair, 1],
                              ALU.subtract).then_inc(hfold_done[pair], 1)

        def fold_p(eng, vec, k):
            for pair in range(2):
                eng.wait_ge(hfold_done[pair], k.count(1, 1))
            if k.first >= 1:
                eng.wait_ge(wfold_done, k.count(2, 0))
            if k.first % QUAD == 0:
                for form in range(2):
                    last = vec.tensor_copy(pf[:, form].rearrange("p v e c -> p e v c"), hf[:, form])
            else:
                for form in range(2):
                    for e in range(2):
                        last = vec.tensor_tensor(pf[:, form, :, e], hf[:, 0, e], hf[:, 1, e],
                                                 ALU.add if form == e else ALU.subtract)
            last.then_inc(pfold_done, 1)

        @block.vector
        def _(dve):
            steps = [0]

            def prep(instruction):
                steps[0] += 1
                instruction.then_inc(prepared, 1)
                dve.wait_ge(prepared, steps[0])

            def prepare():
                nc.vector.memset(minus2l[:, :], -2.0 * LAMBDA).then_inc(prepared, 1)
                nc.vector.memset(spec_hi[BLOCK:BLOCK + 1, :, :, :].bitcast(F32), 1.0).then_inc(prepared, 1)
                nc.vector.memset(hid_hi[BLOCK:BLOCK + 1, :, :, :].bitcast(F32), 1.0).then_inc(prepared, 1)
                steps[0] = 3
                for n in range(2):
                    dve.wait_ge(hconst_in, (n + 1) * DMA)
                    prep(nc.vector.tensor_copy(fh[:, n].rearrange("p b c d -> p (b c d)"), raw_h[:, 0:1024]))
                dve.wait_ge(hconst_in, 3 * DMA)
                prep(nc.vector.tensor_copy(ih[:, :, :, :].rearrange("p a b d -> p (a b d)"), raw_i[:, 0:512]))
                dve.wait_ge(mlp_in, 4 * DMA)
                prep(nc.vector.tensor_scalar(raw_m[BLOCK:BLOCK + 1, 1], raw_m[BLOCK:BLOCK + 1, 1],
                                             LAMBDA, None, ALU.add))
                for n, (mat, order) in enumerate(((m1, (0, 1, 2)), (m2, (1, 0, 2)))):
                    re_at, neg_at, im_at = order
                    raw = raw_m[:, n].rearrange("p (k o t) -> p k o t", k=NBLOCKS, t=2)
                    top, bias = slice(0, BLOCK), slice(BLOCK, BLOCK + 1)
                    for rows, at, t in ((top, re_at, 0), (top, im_at, 1), (bias, 1, 0), (bias, 2, 1)):
                        prep(nc.vector.tensor_copy(mat[rows, 0, :, at], raw[rows, :, :, t]))
                        prep(nc.vector.tensor_tensor(mat[rows, 1, :, at], raw[rows, :, :, t],
                                                     mat[rows, 0, :, at].bitcast(F32), ALU.subtract))
                    for part in range(2):
                        prep(nc.vector.tensor_scalar(mat[top, part, :, neg_at], mat[top, part, :, im_at].bitcast(F32),
                                                     -1.0, None, ALU.mult))
                assert steps[0] == PREPARED

            def fold_w(k, o):
                if o == 0:
                    dve.wait_ge(pfold_done, k.count(1, 1))
                    if k.first >= 2:
                        dve.wait_ge(fwd_mm, k.count(4, -4))
                halves = [pf[:, :, v].rearrange("p f e c -> p f (e c)") for v in range(2)]
                nc.vector.tensor_tensor(wmov[:, k.slot, o], halves[0], halves[1],
                                        ALU.subtract if o else ALU.add).then_inc(wfold_done, 1)

            def fwd_step(k, tile):
                if tile % 2 and k.first + 1 < WUNITS:
                    fold_w(k + 1, tile // 2)

            def split_sin(u, t):
                dve.wait_ge(sin_hi_done, u.count(2, t + 1))
                nc.vector.tensor_tensor(sin_lo[:, u.slot, t], sin[:, u.slot, t], sin_hi[:, u.slot, t].bitcast(F32),
                                        ALU.subtract).then_inc(sin_lo_done, 1)

            def step(u, b):
                n = 2 * u.first + b
                if 3 <= n < STEPS + 3:
                    s = (n - 3) % 2
                    dve.wait_ge(above_done, u.count(2, b - 2))
                    if n >= 5:
                        dve.wait_ge(shr_lo_done, u.count(2, b - 4))
                    nc.vector.scalar_tensor_tensor(shrunk[:, s].rearrange("p e c -> p (e c)"), l2_bank[:, 0:PAIR],
                                                   0.0, above[:, s].rearrange("p e c -> p (e c)"),
                                                   ALU.min, ALU.add).then_inc(shrunk_done, 1)
                if n < STEPS:
                    dve.wait_ge(spec_hi_done, u.count(2, b + 1))
                    nc.vector.tensor_tensor(spec_lo[:, n % 2].rearrange("p t y -> p (t y)"), h_bank[b][0:BLOCK, :],
                                            spec_hi[0:BLOCK, n % 2].rearrange("p t y -> p (t y)").bitcast(F32),
                                            ALU.subtract).then_inc(spec_lo_done, 1)
                if 3 <= n < STEPS + 3:
                    dve.wait_ge(shr_hi_done, u.count(2, b - 2))
                    v, blk = (u - 1, 0) if b else (u - 2, 1)
                    nc.vector.tensor_tensor(shr_lo[:, v.slot, :, blk], shrunk[:, (n - 3) % 2],
                                            shr_hi[:, v.slot, :, blk].bitcast(F32),
                                            ALU.subtract).then_inc(shr_lo_done, 1)
                if u.first + 1 < UNITS:
                    split_sin(u + 1, b)
                if 1 <= n < STEPS + 1:
                    s = (n - 1) % 2
                    dve.wait_ge(hid_hi_done, u.count(2, b))
                    nc.vector.scalar_tensor_tensor(hid_lo[:, s].rearrange("p t y -> p (t y)"), l1_bank[0:BLOCK, :], 0.0,
                                                   hid_hi[0:BLOCK, s].rearrange("p t y -> p (t y)").bitcast(F32),
                                                   ALU.max, ALU.subtract).then_inc(hid_lo_done, 1)

            def unfold_w(j, form):
                dve.wait_ge(vev_done, j.count(2, form + 1))
                dve.wait_ge(inv_mm, j.count(4, 2 * form + 2))
                if form == 0 and j.first >= 1:
                    dve.wait_ge(vp_done, j.count(1, 0 if j.first <= ALONE else -1))
                odd, to = inv_bank(j, 2 * form + 1), vw_of(j)[form]
                nc.vector.tensor_tensor(to[:, 0:PAIR], vev[:, form], odd[:, 0:PAIR], ALU.add)
                nc.vector.tensor_tensor(to[:, PAIR:], vev[:, form], odd[:, 0:PAIR],
                                        ALU.subtract).then_inc(vw_done, 1)

            def unfold_h(j):
                dve.wait_ge(vp_done, j.count(1, 1))
                if j.first >= 2:
                    dve.wait_ge(y_put[j.slot], j.uses(0, 4))
                for hh in range(2):
                    nc.vector.tensor_tensor(yt[:, j.slot, :, hh], vp_of(j)[:, :, :, 0], vp_of(j)[:, :, :, 1],
                                            ALU.subtract if hh else ALU.add).then_inc(yt_rows, 1)

            def add_x(j):
                dve.wait_ge(yt_rows, j.count(2, 2))
                dve.wait_ge(xr_in[j.slot], j.uses(1, 4))
                rows = yt[:, j.slot].rearrange("p a h v c -> p (a h v c)")
                nc.vector.tensor_tensor(rows, rows, xr[:, j.slot].rearrange("p a h v c -> p (a h v c)"),
                                        ALU.add).then_inc(yt_done, 1)

            def inv_step(j, tile):
                if tile % 2 and j.first < WUNITS:
                    unfold_w(j, tile // 2)
                if tile == 2 and 1 <= j.first < WUNITS + 1:
                    unfold_h(j - 1)
                if tile == 0 and j.first >= 2:
                    add_x(j - 2)

            def unit(g, u, reg):
                for b in range(2):
                    step(Index(KX * g + u, reg, SPAN), b)
                    k, tile = forward_at(g, u, b, reg)
                    if k:
                        fwd_step(k, tile)
                    j, tile = inverse_at(g, u, b, reg)
                    if j:
                        inv_step(j, tile)

            def fwd_alone(k):
                for tile in range(4):
                    fwd_step(k, tile)
                    if tile == 0:
                        fold_h(dve, nc.vector, k + 2, 1)
                fold_p(dve, nc.vector, k + 2)

            def inv_alone(j):
                for tile in range(4):
                    inv_step(j, tile)

            fold_h(dve, nc.vector, Index(0), 1)
            fold_p(dve, nc.vector, Index(0))
            for o in range(2):
                fold_w(Index(0), o)
            fold_h(dve, nc.vector, Index(1), 1)
            fold_p(dve, nc.vector, Index(1))
            prepare()
            walk_w(dve, fwd_alone, 0, 2, QUAD - 2, QUAD + LEAD)
            for t in range(2):
                split_sin(Index(0), t)
            walk(dve, unit)
            walk_w(dve, inv_alone, ALONE, ALONE + 2, WUNITS, WUNITS + 2)

        @block.gpsimd
        def _(pool):
            def unfold_p(j):
                pool.wait_ge(vw_done, j.count(2, 2))
                if j.first >= 1:
                    pool.wait_ge(yt_rows, j.count(2, 0 if j.first <= ALONE else -2))
                source, to = vw_of(j), vp_of(j)
                if j.first % QUAD == 0:
                    for pair in range(2):
                        last = nc.gpsimd.tensor_copy(to[:, pair].rearrange("p v e c -> p (v e c)"), source[pair])
                else:
                    c, s = (part.rearrange("p (v e c) -> p v e c", v=2, e=2) for part in source)
                    nc.gpsimd.tensor_tensor(to[:, 0].rearrange("p v e c -> p (v e c)"), *source, ALU.add)
                    nc.gpsimd.tensor_tensor(to[:, 1, :, 0], c[:, :, 0], s[:, :, 0], ALU.subtract)
                    last = nc.gpsimd.tensor_tensor(to[:, 1, :, 1], s[:, :, 1], c[:, :, 1], ALU.subtract)
                last.then_inc(vp_done, 1)

            def unit(g, u, reg):
                for b in range(2):
                    k, tile = forward_at(g, u, b, reg)
                    if k and tile == 0 and k.first + 2 < WUNITS:
                        for pair in range(2):
                            fold_h(pool, nc.gpsimd, k + 2, pair)
                        fold_p(pool, nc.gpsimd, k + 2)
                    j, tile = inverse_at(g, u, b, reg)
                    if j and tile == 3:
                        unfold_p(j)

            walk_w(pool, lambda k: fold_h(pool, nc.gpsimd, k, 0), 0, 2, QUAD + LEAD, QUAD + LEAD + 2)
            walk(pool, unit)
            walk_w(pool, unfold_p, ALONE, ALONE + 2, WUNITS, WUNITS)


PREPARED = 27


def dft_constants():
    def twelve(v):
        m, e = np.frexp(v)
        return np.ldexp(np.rint(m * 4096.0) / 4096.0, e)

    def parts(a):
        hi = twelve(a)
        return np.ascontiguousarray(np.stack([hi, twelve(a - hi)], axis=1).astype(np.float32))

    i = np.arange(HALF)
    scale = 1.0 / np.sqrt(SIDE)
    fwd_w, inv_w = np.zeros((HALF, 2, 128)), np.zeros((128, 2, 2, HALF))
    fwd_h, inv_h = np.zeros((128, 2, 4, HALF)), np.zeros((HALF, 2, 128))
    row = np.arange(128)
    for parity in range(2):
        angle = 2 * np.pi * (np.outer(i, 2 * i + parity) % SIDE) / SIDE
        cos, sin = scale * np.cos(angle), scale * np.sin(angle)
        k = QUAD
        fwd_w[:, parity, :k], fwd_w[:, parity, k:] = cos[:, :k], -sin[:, :k]
        inv_w[:k, 0, parity], inv_w[k:, 0, parity] = 2 * cos[:, :k].T, -2 * sin[:, :k].T
        at = np.where(row > 64, row - 64, row)
        is_cos = (row < 64) | ((row == 64) & (parity == 0))
        c, s = cos[at] * is_cos[:, None], sin[at] * ~is_cos[:, None]
        fwd_h[:, parity, 0], fwd_h[:, parity, 1], fwd_h[:, parity, 2], fwd_h[:, parity, 3] = c + s, c - s, c, -s
        inv_h[:, parity] = (c + s).T
    nyquist = scale * (1.0 - 2.0 * (i % 2))
    fwd_w[:, 0, 64] = nyquist
    inv_w[0, 0, 0], inv_w[64, 0, 0] = scale, nyquist
    inv_w[:, 1] = inv_w[:, 0]
    inv_w[0:64, 1] *= -1.0
    inv_w[64, 1, 0] *= -1.0
    fwd_h, inv_h = parts(fwd_h), parts(inv_h)
    return (fwd_w.astype(np.float32), inv_w.astype(np.float32),
            fwd_h.reshape(128, 2, -1), inv_h.reshape(128, -1))


def kernel(**inputs):
    import concourse.bacc as bacc
    from concourse.bass_utils import run_bass_kernel_spmd

    nc = bacc.Bacc("TRN2", target_bir_lowering=False, num_devices=1)
    fwd_w, inv_w, fwd_h, inv_h = dft_constants()
    arrays = {name: np.ascontiguousarray(inputs[name]) for name in
              ("x", "L0_conv_w1", "L0_conv_b1", "L0_conv_w2", "L0_conv_b2")}
    arrays.update(fwd_w=fwd_w, inv_w=inv_w, fwd_h=fwd_h, inv_h=inv_h)
    args = [nc.dram_tensor("in_" + name, a.shape, mybir.dt.from_np(a.dtype), kind="ExternalInput").ap()
            for name, a in arrays.items()]
    out = nc.dram_tensor("out_dram", arrays["x"].shape, F32, kind="ExternalOutput").ap()
    spectral_conv(nc, *args, out)
    result = run_bass_kernel_spmd(nc, [{"in_" + name: a for name, a in arrays.items()}], core_ids=[0])
    return result.results[0]["out_dram"]
```

```python
from contextlib import ExitStack

import numpy as np

import concourse.bass as bass
from concourse import mybir

ALU = mybir.AluOpType
ACT = mybir.ActivationFunctionType
F32 = mybir.dt.float32
F32R = mybir.dt.float32r

LAMBDA = float(np.float32(0.01))
SIDE = 256
HALF = SIDE // 2
CHANNELS = 768
BLOCK = 96
NBLOCKS = CHANNELS // BLOCK
GROUPS = 4
GC = CHANNELS // GROUPS
PAIR = 2 * GC
KX = HALF + 1
UNITS = GROUPS * KX
STEPS = 2 * UNITS
QUAD = HALF // 2
WUNITS = GROUPS * QUAD
PITCH = HALF * PAIR + 1024
LEAD = 2
LAG = 5
DMA = 16
SPAN = 8
LOOP_FROM, LOOPS = 12, 13
SP_FROM, SP_LOOPS = 14, 13
BESIDE = QUAD + LEAD
ALONE = WUNITS - QUAD
SIN_SLOTS = 4


class Index:

    def __init__(self, first, reg=None, stride=0):
        self.first, self.reg, self.stride, self.slot = first, reg, stride, first % 2

    def count(self, times=1, plus=0):
        value = times * self.first + plus
        return value if self.reg is None else self.reg * (times * self.stride) + value

    def uses(self, plus, dmas, slots=2):
        value = dmas * DMA * (self.first // slots + plus)
        return value if self.reg is None else self.reg * (dmas * DMA * self.stride // slots) + value

    def __add__(self, n):
        return Index(self.first + n, self.reg, self.stride)

    def __sub__(self, n):
        return self + -n


def group_of(unit):
    return unit // KX


def forward_at(g, u, b, reg, late=1):
    pos = 2 * u + b + 4 * LEAD - late
    if g < GROUPS - 1 and LEAD <= pos // 4 < QUAD + LEAD:
        return Index(QUAD * (g + 1) + pos // 4, reg, SPAN // 2), pos % 4
    return None, 0


def inverse_at(g, u, b, reg, late=1):
    pos = 2 * (u - LAG) + b - late
    if g >= 1 and 0 <= pos < 4 * QUAD:
        return Index(QUAD * (g - 1) + pos // 4, reg, SPAN // 2), pos % 4
    pos += 2 * KX
    if g >= 2 and pos < 4 * QUAD:
        return Index(QUAD * (g - 2) + pos // 4, reg, SPAN // 2), pos % 4
    return None, 0


def walk(engine, unit, loop_from=LOOP_FROM, loops=LOOPS):
    for g in range(GROUPS):
        last = KX if g < GROUPS - 1 else (4 * QUAD) // 2 + LAG + 1
        for u in range(loop_from):
            unit(g, u, None)
        with engine.Fori(0, loops) as r:
            for u in range(loop_from, loop_from + SPAN):
                unit(g, u, r)
        for u in range(loop_from + SPAN * loops, last):
            unit(g, u, None)


def walk_w(engine, unit, first, start, end, last):
    for k in range(first, start):
        unit(Index(k))
    with engine.Fori(0, (end - start) // 2) as r:
        for k in range(start, start + 2):
            unit(Index(k, r, 2))
    for k in range(end, last):
        unit(Index(k))


def spectral_conv(nc, x, w1, b1, w2, b2, fwd_w, inv_w, fwd_h, inv_h, out):
    s1 = nc.dram_tensor("s1_scratch", (GROUPS, 2, HALF, PITCH), F32, kind="Internal").ap()
    s2 = nc.dram_tensor("s2_scratch", (GROUPS, 2, HALF, PITCH), F32, kind="Internal").ap()

    with ExitStack() as ctx:
        def sb(name, shape, dt=F32):
            return ctx.enter_context(nc.sbuf_tensor(name, shape, dt))

        def ps(name):
            return ctx.enter_context(nc.psum_tensor(name, [128, 512], F32))

        def sem(name):
            return ctx.enter_context(nc.semaphore(name))

        xt = sb("xt", [128, 2, 2, 2, 2, GC])
        hf = sb("hf", [128, 2, 2, 2, GC])
        pf = sb("pf", [128, 2, 2, 2, GC])
        wmov = sb("wmov", [128, 2, 2, 2, PAIR])
        wout = sb("wout", [128, 2, 2, 2, PAIR])
        wmov_hi = sb("wmov_hi", [128, 2, PAIR], F32R)
        wmov_lo = sb("wmov_lo", [128, 2, PAIR], F32R)
        vmov = sb("vmov", [128, 2, 2, 2, PAIR])
        vmov_hi = sb("vmov_hi", [128, 2, PAIR], F32R)
        vmov_lo = sb("vmov_lo", [128, 2, PAIR], F32R)
        xr = sb("xr", [128, 2, 2, 2, 2, GC])
        vev = sb("vev", [128, 2, PAIR])
        vw = sb("vw", [128, 2, 2, PAIR])
        vp = sb("vp", [128, 2, 2, 2, GC])
        yt = sb("yt", [128, 2, 2, 2, 2, GC])
        sin = sb("sin", [128, SIN_SLOTS, 2, PAIR])
        spec_hi = sb("spec_hi", [BLOCK + 1, 2, 2, SIDE], F32R)
        spec_lo = sb("spec_lo", [BLOCK, 2, 2, SIDE], F32R)
        hid = sb("hid", [BLOCK + 1, 2, 2, SIDE])
        above = sb("above", [128, 2, 2, 2 * BLOCK])
        shrunk = sb("shrunk", [128, 2, 2, 2 * BLOCK])
        shr_hi = sb("shr_hi", [128, 2, 2, 2, 2 * BLOCK], F32R)
        shr_lo = sb("shr_lo", [128, 2, 2, 2, 2 * BLOCK], F32R)
        sout = sb("sout", [128, 2, 2, 2, GC])
        fw = sb("fw", [128, 2, 128])
        iw = sb("iw", [128, 2, 2, 128])
        fw_parts = sb("fw_parts", [128, 2, 2, 128], F32R)
        iw_parts = sb("iw_parts", [128, 2, 2, 2, 128], F32R)
        fh = sb("fh", [128, 2, 4, 128])
        ih = sb("ih", [128, 2, 2, 128], F32R)
        m1 = sb("m1", [BLOCK + 1, 2, NBLOCKS, 3, BLOCK], F32R)
        m2 = sb("m2", [BLOCK + 1, NBLOCKS, 3, BLOCK])
        minus2l = sb("minus2l", [128, 1])

        h_bank = [ps("h_bank0"), ps("h_bank1")]
        l1_bank, l2_bank = ps("l1_bank"), ps("l2_bank")
        ih_bank = [ps("ih_even"), ps("ih_odd")]
        fwd_beside, inv_beside = ps("fwd_bank"), ps("inv_bank")

        wconst_in, hconst_in, mlp_in = sem("wconst_in"), sem("hconst_in"), sem("mlp_in")
        prepared = sem("prepared")
        x_in = [sem("x_in0"), sem("x_in1")]
        hfold_done = [sem("hfold0_done"), sem("hfold1_done")]
        pfold_done = sem("pfold_done")
        wfold_done = sem("wfold_done")
        fwd_hi_done, fwd_lo_done = sem("fwd_hi_done"), sem("fwd_lo_done")
        fwd_mm = sem("fwd_mm")
        fwd_out = sem("fwd_out")
        s1_put = [sem("s1_put0"), sem("s1_put1")]
        s1_edge = sem("s1_edge")
        sin_in = [sem("sin_in%d" % i) for i in range(SIN_SLOTS)]
        h_mm, l1_mm, l2_mm = sem("h_mm"), sem("l1_mm"), sem("l2_mm")
        spec_hi_done, spec_lo_done = sem("spec_hi_done"), sem("spec_lo_done")
        hid_done = sem("hid_done")
        above_done, shrunk_done = sem("above_done"), sem("shrunk_done")
        shr_hi_done, shr_lo_done = sem("shr_hi_done"), sem("shr_lo_done")
        ih_mm, ih_out = sem("ih_mm"), sem("ih_out")
        s2_put = [sem("s2_put0"), sem("s2_put1")]
        s2_edge = [sem("s2_edge0"), sem("s2_edge1")]
        v_in = [sem("v_in0"), sem("v_in1")]
        v_edge = sem("v_edge")
        xr_in = [sem("xr_in0"), sem("xr_in1")]
        inv_hi_done, inv_lo_done = sem("inv_hi_done"), sem("inv_lo_done")
        inv_mm = sem("inv_mm")
        vev_done = sem("vev_done")
        vw_done = sem("vw_done")
        vp_done = sem("vp_done")
        yt_rows = sem("yt_rows")
        yt_done = sem("yt_done")
        y_put = [sem("y_put0"), sem("y_put1")]

        raw_i = vw[:, :, :, :].rearrange("p a b c -> p (a b c)")
        raw_m = xr[:, :, :, :, :, :].rearrange("p s a b v c -> p s (a b v c)")

        def tile_of(scratch, g, t, q):
            return scratch[g, t, q, 0:HALF * PAIR].rearrange("(h c) -> h c", h=HALF)

        def slots_of(scratch, g, t, row):
            return scratch[g, t].rearrange("(o k) c -> k o c", o=2)[:, :, bass.ts(row, PAIR)]

        def local(k):
            return k.count(1, -QUAD * (k.first // QUAD))

        def mirrored(k):
            if k.first % QUAD == 0:
                return HALF // 2
            value = HALF - k.first % QUAD
            return value if k.reg is None else k.reg * -k.stride + value

        def fwd_bank(k, tile):
            return fwd_beside if k.first >= BESIDE else [fwd_beside, inv_beside, *h_bank][tile]

        def inv_bank(j, tile):
            if j.first < ALONE:
                return inv_beside
            return [[inv_beside, fwd_beside, *h_bank], [l1_bank, l2_bank, *ih_bank]][j.slot][tile]

        def vw_of(j):
            if j.first >= ALONE and j.slot:
                return [part[:, :, :, :].rearrange("p v e c -> p (v e c)") for part in (above, shrunk)]
            return [vw[:, form].rearrange("p v c -> p (v c)") for form in range(2)]

        def vp_of(j):
            return sout[:, :, :, :, :] if j.first >= ALONE and j.slot else vp[:, :, :, :, :]

        def store_s1(queue, k, halves=(0, 1)):
            queue.wait_ge(fwd_out, k.count(4, 4))
            g = k.first // QUAD
            for t in halves:
                part = slice(64 * t, 64 * t + 64)
                queue.dma_start(slots_of(s1, g, t, local(k)), wout[part, k.slot, :, 0]) \
                    .then_inc(s1_put[k.slot], DMA)
                if k.first % QUAD:
                    queue.dma_start(slots_of(s1, g, 1 - t, local(k) + QUAD), wout[part, k.slot, :, 1]) \
                        .then_inc(s1_put[k.slot], DMA)
                else:
                    queue.dma_start(slots_of(s1, g, t, QUAD)[:, :, 0:GC], wout[part, k.slot, :, 1, 0:GC]) \
                        .then_inc(s1_put[k.slot], DMA)
                    queue.dma_start(slots_of(s1, g, 1 - t, QUAD)[:, :, GC:], wout[part, k.slot, :, 1, GC:]) \
                        .then_inc(s1_edge, DMA)

        def store_y(queue, j):
            queue.wait_ge(yt_done, j.count(1, 1))
            for pair in range(2):
                for hh in range(2):
                    queue.dma_start(image(out, j, pair, hh), yt[:, j.slot, pair, hh]).then_inc(y_put[j.slot], DMA)

        def image(a, k, pair, hh):
            g = k.first // QUAD
            row = a[0, HALF * hh:HALF * (hh + 1)][mirrored(k) if pair else local(k)]
            return row.rearrange("(v w) c -> w v c", v=2)[:, :, g * GC:(g + 1) * GC]

        block = ctx.enter_context(nc.Block())

        @block.sync
        def _(sp):
            def load_rows(tile, k, landed):
                for pair in range(2):
                    for hh in range(2):
                        sp.dma_start(tile[:, k.slot, pair, hh], image(x, k, pair, hh)).then_inc(landed[k.slot], DMA)

            def fwd_unit(k):
                if k.first + 3 < WUNITS:
                    for pair in range(2):
                        sp.wait_ge(hfold_done[pair], k.count(1, 2))
                    load_rows(xt, k + 3, x_in)
                if 1 <= k.first < WUNITS + 1:
                    store_s1(sp, k - 1, (0,) if k.first <= BESIDE else (0, 1))

            def load_sin(u):
                g = group_of(u.first)
                v = u.first - KX * g
                if v == 0:
                    for s in range(2):
                        sp.wait_ge(s1_put[s], 4 * DMA * QUAD // 2 * (g + 1))
                    sp.wait_ge(s1_edge, 2 * DMA * (g + 1))
                slot = u.first % SIN_SLOTS
                if u.first >= SIN_SLOTS:
                    sp.wait_ge(h_mm, u.count(2, 2 - 2 * SIN_SLOTS))
                for t in (1, 0):
                    sp.dma_start(sin[:, slot, t], tile_of(s1, g, t, 0 if v < 2 else u.count(1, -1 - KX * g))) \
                        .then_inc(sin_in[slot], DMA)

            def store_s2(u):
                g = group_of(u.first)
                v = u.first - KX * g
                sp.wait_ge(ih_out, u.count(2, 2))
                if v >= 2:
                    for t in range(2):
                        sp.dma_start(tile_of(s2, g, t, u.count(1, -1 - KX * g)),
                                     sout[:, u.slot, t].rearrange("p e c -> p (e c)")).then_inc(s2_put[u.slot], DMA)
                    return
                re_at, im_at = tile_of(s2, g, v, 0), tile_of(s2, g, 1 - v, 0)
                sp.dma_start(re_at[0:64], sout[0:64, u.slot, 0].rearrange("p e c -> p (e c)")) \
                    .then_inc(s2_put[u.slot], DMA)
                sp.dma_start(im_at[65:128], sout[65:128, u.slot, 1].rearrange("p e c -> p (e c)")) \
                    .then_inc(s2_put[u.slot], DMA)
                sp.dma_start(re_at[64:65, 0:GC], sout[64:65, u.slot, 0, 0]).then_inc(s2_edge[u.slot], DMA)
                sp.dma_start(im_at[64:65, GC:], sout[64:65, u.slot, 1, 1]).then_inc(s2_edge[u.slot], DMA)

            def load_vmov(j):
                g = j.first // QUAD
                if j.first % QUAD == 0:
                    for s in range(2):
                        sp.wait_ge(s2_put[s], 2 * DMA * ((KX * (g + 1) + 1 - s) // 2))
                        sp.wait_ge(s2_edge[s], 2 * DMA * (g + 1))
                if j.first >= 2:
                    sp.wait_ge(inv_mm if j.first >= ALONE + 2 else inv_lo_done, j.count(4, -4))
                for t in (1, 0):
                    part = slice(64 * t, 64 * t + 64)
                    sp.dma_start(vmov[part, j.slot, 0], slots_of(s2, g, t, local(j))).then_inc(v_in[j.slot], DMA)
                    if j.first % QUAD:
                        sp.dma_start(vmov[part, j.slot, 1], slots_of(s2, g, 1 - t, local(j) + QUAD)) \
                            .then_inc(v_in[j.slot], DMA)
                    else:
                        sp.dma_start(vmov[part, j.slot, 1, :, 0:GC], slots_of(s2, g, t, QUAD)[:, :, 0:GC]) \
                            .then_inc(v_in[j.slot], DMA)
                        sp.dma_start(vmov[part, j.slot, 1, :, GC:], slots_of(s2, g, 1 - t, QUAD)[:, :, GC:]) \
                            .then_inc(v_edge, DMA)

            def inv_unit(j):
                if (j.first + 1) % QUAD and j.first < WUNITS:
                    load_vmov(j + 1)
                if 1 <= j.first < WUNITS + 1:
                    if j.first >= 3:
                        sp.wait_ge(yt_done, j.count(1, -2))
                    load_rows(xr, j - 1, xr_in)
                if 3 <= j.first < ALONE:
                    store_y(sp, j - 3)

            def unit(g, u, reg):
                at = Index(KX * g + u, reg, SPAN)
                if at.first + 2 < UNITS:
                    load_sin(at + 2)
                if 4 <= at.first < UNITS + 4:
                    store_s2(at - 4)
                for b in range(2):
                    k, tile = forward_at(g, u, b, reg)
                    if k and tile == 0:
                        fwd_unit(k)
                    j, tile = inverse_at(g, u, b, reg)
                    if j and tile == 0:
                        inv_unit(j)
                if u == LAG - 1 and g >= 1:
                    load_vmov(Index(QUAD * (g - 1)))

            sp.dma_start(fw[:, :, :], fwd_w).then_inc(wconst_in, DMA)
            for k in range(2):
                load_rows(xt, Index(k), x_in)
            for n, (w, b) in enumerate(((w1, b1), (w2, b2))):
                sp.dma_start(raw_m[0:BLOCK, n].rearrange("p (k o) -> p k o", k=NBLOCKS),
                             w.rearrange("k i o t -> i k (o t)")).then_inc(mlp_in, DMA)
                sp.dma_start(raw_m[BLOCK:BLOCK + 1, n], b.rearrange("(z k) o t -> z (k o t)", z=1)) \
                    .then_inc(mlp_in, DMA)
            sp.dma_start(fh[:, :, :, :], fwd_h).then_inc(hconst_in, DMA)
            sp.dma_start(raw_i[:, 0:512], inv_h).then_inc(hconst_in, DMA)
            sp.dma_start(iw[:, :, :, :], inv_w).then_inc(wconst_in, DMA)
            for pair in range(2):
                sp.wait_ge(hfold_done[pair], 1)
            load_rows(xt, Index(2), x_in)

            walk_w(sp, fwd_unit, 0, 2, QUAD - 4, BESIDE)
            sp.wait_ge(prepared, PREPARED)
            load_sin(Index(0))
            load_sin(Index(1))
            walk(sp, unit, SP_FROM, SP_LOOPS)
            load_vmov(Index(ALONE))
            walk_w(sp, inv_unit, ALONE, ALONE + 2, WUNITS - 2, WUNITS + 1)
            for s in range(2):
                sp.wait_ge(y_put[s], 4 * DMA * WUNITS // 2)

        @block.tensor
        def _(pe):
            def forward_h(u, b):
                n = 2 * u.first + b
                slot = u.first % SIN_SLOTS
                if b == 0:
                    pe.wait_ge(sin_in[slot], u.uses(1, 2, SIN_SLOTS))
                if n >= 2:
                    pe.wait_ge(spec_lo_done, u.count(2, b - 1))
                v = u.first - KX * group_of(u.first)
                plan = {0: ((0, 2), (1, 3)), 1: ((1, 2), (0, 3))}.get(v, ((0, 0), (1, 1)))
                for e in range(2):
                    cols = slice(e * GC + b * BLOCK, e * GC + (b + 1) * BLOCK)
                    for t, (tile, matrix) in enumerate(plan):
                        bank = h_bank[b][0:BLOCK, t * SIDE + e * HALF:t * SIDE + (e + 1) * HALF]
                        mm = nc.tensor.matmul(bank, sin[:, slot, tile, cols], fh[:, e, matrix],
                                              start=True, stop=True)
                mm.then_inc(h_mm, 1)

            def layer1(u, b):
                i = 2 * u.first + b - 1
                blk, s = 2 * group_of(i // 2) + i % 2, i % 2
                pe.wait_ge(spec_lo_done, u.count(2, b))
                if i >= 1:
                    pe.wait_ge(hid_done, u.count(2, b - 1))
                both = l1_bank[0:BLOCK, :]
                for p, (data, part, bias) in enumerate(((spec_hi, 0, 1), (spec_hi, 1, 1), (spec_lo, 0, 0))):
                    rows = BLOCK + bias
                    if p < 2:
                        nc.tensor.matmul(both, m1[0:BLOCK, part, blk, 0], data[0:BLOCK, s], start=p == 0, stop=False)
                    nc.tensor.matmul(both[:, 0:SIDE], m1[0:rows, part, blk, 1], data[0:rows, s, 1],
                                     start=False, stop=False)
                    nc.tensor.matmul(both[:, SIDE:], m1[0:rows, part, blk, 2], data[0:rows, s, 0],
                                     start=False, stop=False)
                nc.tensor.matmul(both, m1[0:BLOCK, 0, blk, 0], spec_lo[0:BLOCK, s], start=False, stop=True) \
                    .then_inc(l1_mm, 1)

            def layer2(u, b):
                i = 2 * u.first + b - 2
                blk, s = 2 * group_of(i // 2) + i % 2, i % 2
                pe.wait_ge(hid_done, u.count(2, b - 1))
                if i >= 1:
                    pe.wait_ge(shrunk_done, u.count(2, b - 2))
                for e in range(2):
                    bank = l2_bank[:, e * 2 * BLOCK:(e + 1) * 2 * BLOCK]
                    ky = slice(e * HALF, (e + 1) * HALF)
                    nc.tensor.matmul(bank, hid[:, s, 0, ky], m2[:, blk, 1:3], start=True, stop=False)
                    mm = nc.tensor.matmul(bank, hid[0:BLOCK, s, 1, ky], m2[0:BLOCK, blk, 0:2],
                                          start=False, stop=True)
                mm.then_inc(l2_mm, 1)

            def inverse_h(u, b):
                v, e = (u - 2, 0) if b else (u - 3, 1)
                if e == 0:
                    pe.wait_ge(shr_lo_done, v.count(2, 2))
                if v.first >= 1:
                    pe.wait_ge(ih_out, v.count(2, e - 1))
                for p, (part, data) in enumerate(((0, shr_hi), (1, shr_hi), (0, shr_lo))):
                    mm = nc.tensor.matmul(ih_bank[e][:, 0:PAIR], ih[:, part, e], data[:, v.slot, e],
                                          start=p == 0, stop=p == 2)
                mm.then_inc(ih_mm, 1)

            def fwd_tile(k, tile):
                bank = fwd_bank(k, tile)[:, 0:PAIR]
                if k.first < BESIDE:
                    if tile == 0:
                        pe.wait_ge(wfold_done, k.count(2, 2))
                    if k.first >= 1:
                        pe.wait_ge(fwd_out, k.count(4, tile - 3))
                    nc.tensor.matmul(bank, fw[:, tile // 2], wmov[:, k.slot, tile // 2, tile % 2],
                                     start=True, stop=True).then_inc(fwd_mm, 1)
                    return
                pe.wait_ge(fwd_lo_done, k.count(4, tile + 1 - 4 * BESIDE))
                pe.wait_ge(fwd_out, k.count(4, tile))
                for p, (data, part) in enumerate(((wmov_hi, 0), (wmov_hi, 1), (wmov_lo, 0))):
                    mm = nc.tensor.matmul(bank, fw_parts[:, part, tile // 2], data[:, tile % 2],
                                          start=p == 0, stop=p == 2)
                mm.then_inc(fwd_mm, 1)

            def inv_tile(j, tile):
                form, o = tile // 2, tile % 2
                bank = inv_bank(j, tile)
                alone = j.first >= ALONE
                if alone:
                    if tile == 0:
                        pe.wait_ge(v_in[j.slot], j.uses(1, 4))
                    if j.first >= ALONE + 2:
                        pe.wait_ge(vw_done if o else vev_done, j.count(2, form - 3))
                else:
                    pe.wait_ge(inv_lo_done, j.count(4, tile + 1))
                    if o:
                        pe.wait_ge(vev_done, j.count(2, form + 1))
                    elif 2 * j.first + form >= 1:
                        pe.wait_ge(vw_done, j.count(2, form))
                lone = form == 1 and j.first % QUAD == 0
                if alone and lone and o == 0:
                    pe.wait_ge(v_edge, 2 * DMA * (j.first // QUAD + 1))
                for cols, rows in (((slice(0, GC), 0), (slice(GC, PAIR), 1)) if lone else ((slice(0, PAIR), form),)):
                    if alone:
                        mm = nc.tensor.matmul(bank[:, cols], iw[:, rows, o], vmov[:, j.slot, form, o, cols],
                                              start=True, stop=True)
                        continue
                    for p, (data, part) in enumerate(((vmov_hi, 0), (vmov_hi, 1), (vmov_lo, 0))):
                        mm = nc.tensor.matmul(bank[:, cols], iw_parts[:, part, rows, o], data[:, tile % 2, cols],
                                              start=p == 0, stop=p == 2)
                mm.then_inc(inv_mm, 1)

            def unit(g, u, reg):
                at = Index(KX * g + u, reg, SPAN)
                for b in range(2):
                    n = 2 * at.first + b
                    if n < STEPS:
                        forward_h(at, b)
                    if 1 <= n < STEPS + 1:
                        layer1(at, b)
                    if 5 <= n < STEPS + 5:
                        inverse_h(at, b)
                    k, tile = forward_at(g, u, b, reg)
                    if k and k.first < WUNITS:
                        fwd_tile(k, tile)
                    j, tile = inverse_at(g, u, b, reg)
                    if j:
                        inv_tile(j, tile)
                    if 2 <= n < STEPS + 2:
                        layer2(at, b)

            def fwd_alone(k):
                for tile in range(4):
                    fwd_tile(k, tile)

            def inv_alone(j):
                for tile in range(4):
                    inv_tile(j, tile)

            pe.wait_ge(wconst_in, 2 * DMA)
            walk_w(pe, fwd_alone, 0, 2, QUAD, BESIDE)
            pe.wait_ge(prepared, PREPARED)
            pe.wait_ge(fwd_out, 4 * BESIDE)
            walk(pe, unit)
            pe.wait_ge(vw_done, 2 * ALONE)
            pe.wait_ge(fwd_out, 4 * WUNITS)
            pe.wait_ge(shrunk_done, STEPS)
            pe.wait_ge(ih_out, STEPS)
            walk_w(pe, inv_alone, ALONE, ALONE + 2, WUNITS, WUNITS)

        @block.scalar
        def _(act):
            def fwd_out_tile(k, tile):
                act.wait_ge(fwd_mm, k.count(4, tile + 1))
                if tile == 0 and k.first >= 2:
                    act.wait_ge(s1_put[k.slot], k.uses(0, 4))
                    if k.first % QUAD == 2:
                        act.wait_ge(s1_edge, 2 * DMA * (k.first // QUAD + 1))
                nc.scalar.activation(wout[:, k.slot, tile // 2, tile % 2], fwd_bank(k, tile)[:, 0:PAIR],
                                     ACT.Copy).then_inc(fwd_out, 1)

            def inv_even(j, form):
                act.wait_ge(inv_mm, j.count(4, 2 * form + 1))
                if j.first >= 1:
                    act.wait_ge(vw_done, j.count(2, form - 1))
                nc.scalar.activation(vev[:, form], inv_bank(j, 2 * form)[:, 0:PAIR], ACT.Copy).then_inc(vev_done, 1)

            def split_fwd(k, tile):
                act.wait_ge(wfold_done, k.count(2, tile // 2 + 1))
                act.wait_ge(fwd_mm, k.count(4, tile - 1))
                nc.scalar.activation(wmov_hi[:, tile % 2], wmov[:, k.slot, tile // 2, tile % 2],
                                     ACT.Copy).then_inc(fwd_hi_done, 1)

            def split_inv(j, tile):
                if tile == 0:
                    act.wait_ge(v_in[j.slot], j.uses(1, 4))
                if tile == 2 and j.first % QUAD == 0:
                    act.wait_ge(v_edge, 2 * DMA * (j.first // QUAD + 1))
                if 4 * j.first + tile >= 2:
                    act.wait_ge(inv_mm, j.count(4, tile - 1))
                nc.scalar.activation(vmov_hi[:, tile % 2], vmov[:, j.slot, tile // 2, tile % 2],
                                     ACT.Copy).then_inc(inv_hi_done, 1)

            def step(u, b):
                n = 2 * u.first + b
                if 3 <= n < STEPS + 3:
                    act.wait_ge(l2_mm, u.count(2, b - 2))
                    if n >= 5:
                        act.wait_ge(shrunk_done, u.count(2, b - 4))
                    nc.scalar.activation(above[:, (n - 3) % 2].rearrange("p e c -> p (e c)"),
                                         l2_bank[:, 0:PAIR], ACT.Relu, bias=minus2l[:, 0:1]).then_inc(above_done, 1)
                if n < STEPS:
                    act.wait_ge(h_mm, u.count(2, b + 1))
                    if n >= 2:
                        act.wait_ge(l1_mm, u.count(2, b - 1))
                    nc.scalar.activation(spec_hi[0:BLOCK, n % 2].rearrange("p t y -> p (t y)"),
                                         h_bank[b][0:BLOCK, :], ACT.Copy).then_inc(spec_hi_done, 1)
                if 6 <= n < STEPS + 6:
                    v = u - 3
                    act.wait_ge(ih_mm, v.count(2, b + 1))
                    if b == 0 and v.first >= 2:
                        act.wait_ge(s2_put[v.slot], v.uses(0, 2))
                        g = group_of(v.first)
                        if 2 <= v.first - KX * g < 4:
                            act.wait_ge(s2_edge[v.slot], 2 * DMA * (g + 1))
                    nc.scalar.activation(sout[:, v.slot, :, b].rearrange("p t (k c) -> p k t c", k=2),
                                         ih_bank[b][:, 0:PAIR].rearrange("p (k t c) -> p k t c", k=2, t=2),
                                         ACT.Copy).then_inc(ih_out, 1)
                if 3 <= n < STEPS + 3:
                    act.wait_ge(shrunk_done, u.count(2, b - 2))
                    v, blk = (u - 1, 0) if b else (u - 2, 1)
                    if blk == 0 and v.first >= 2:
                        act.wait_ge(ih_mm, v.count(2, -2))
                    nc.scalar.activation(shr_hi[:, v.slot, :, blk], shrunk[:, (n - 3) % 2],
                                         ACT.Copy).then_inc(shr_hi_done, 1)
                if 1 <= n < STEPS + 1:
                    act.wait_ge(l1_mm, u.count(2, b))
                    if n >= 3:
                        act.wait_ge(l2_mm, u.count(2, b - 2))
                    nc.scalar.activation(hid[0:BLOCK, (n - 1) % 2].rearrange("p t y -> p (t y)"),
                                         l1_bank[0:BLOCK, :], ACT.Relu).then_inc(hid_done, 1)

            def unit(g, u, reg):
                for b in range(2):
                    step(Index(KX * g + u, reg, SPAN), b)
                    k, tile = forward_at(g, u, b, reg)
                    if k and k.first < WUNITS:
                        fwd_out_tile(k, tile)
                    j, tile = inverse_at(g, u, b, reg)
                    if j and tile % 2 == 0:
                        inv_even(j, tile // 2)
                    k, tile = forward_at(g, u, b, reg, late=0)
                    if k and k.first < WUNITS:
                        split_fwd(k, tile)
                    j, tile = inverse_at(g, u, b, reg, late=0)
                    if j:
                        split_inv(j, tile)

            def fwd_alone(k):
                for tile in range(4):
                    fwd_out_tile(k, tile)
                store_s1(act, k, (1,))

            def inv_alone(j):
                if j.first < WUNITS:
                    for form in range(2):
                        inv_even(j, form)
                store_y(act, j - 2)

            walk_w(act, fwd_alone, 0, 4, QUAD, BESIDE)
            act.wait_ge(prepared, PREPARED)
            walk(act, unit)
            store_y(act, Index(ALONE - 3))
            walk_w(act, inv_alone, ALONE, ALONE + 4, WUNITS, WUNITS + 2)

        def fold_h(eng, vec, k, pair):
            eng.wait_ge(x_in[k.slot], k.uses(1, 4))
            if k.first >= 1:
                eng.wait_ge(pfold_done, k.count(1, 0))
            vec.tensor_tensor(hf[:, pair, 0], xt[:, k.slot, pair, 0], xt[:, k.slot, pair, 1], ALU.add)
            vec.tensor_tensor(hf[:, pair, 1], xt[:, k.slot, pair, 0], xt[:, k.slot, pair, 1],
                              ALU.subtract).then_inc(hfold_done[pair], 1)

        def fold_p(eng, vec, k):
            for pair in range(2):
                eng.wait_ge(hfold_done[pair], k.count(1, 1))
            if k.first >= 1:
                eng.wait_ge(wfold_done, k.count(2, 0))
            if k.first % QUAD == 0:
                for form in range(2):
                    last = vec.tensor_copy(pf[:, form].rearrange("p v e c -> p e v c"), hf[:, form])
            else:
                for form in range(2):
                    for e in range(2):
                        last = vec.tensor_tensor(pf[:, form, :, e], hf[:, 0, e], hf[:, 1, e],
                                                 ALU.add if form == e else ALU.subtract)
            last.then_inc(pfold_done, 1)

        @block.vector
        def _(dve):
            steps = [0]

            def prep(instruction):
                steps[0] += 1
                instruction.then_inc(prepared, 1)
                dve.wait_ge(prepared, steps[0])

            def prepare_ones():
                nc.vector.memset(minus2l[:, :], -2.0 * LAMBDA).then_inc(prepared, 1)
                nc.vector.memset(spec_hi[BLOCK:BLOCK + 1, :, :, :].bitcast(F32), 1.0).then_inc(prepared, 1)
                nc.vector.memset(hid[BLOCK:BLOCK + 1, :, :, :], 1.0).then_inc(prepared, 1)
                steps[0] = 3

            def prepare():
                dve.wait_ge(hconst_in, 2 * DMA)
                prep(nc.vector.tensor_copy(ih[:, :, :, :].rearrange("p a b d -> p (a b d)"), raw_i[:, 0:512]))
                dve.wait_ge(wconst_in, 2 * DMA)
                fw_all, iw_all = fw.rearrange("p o s -> p (o s)"), iw.rearrange("p f o w -> p (f o w)")
                for whole, parts in ((fw_all, fw_parts.rearrange("p a o s -> p a (o s)")),
                                     (iw_all, iw_parts.rearrange("p a f o w -> p a (f o w)"))):
                    prep(nc.vector.tensor_copy(parts[:, 0], whole))
                    prep(nc.vector.tensor_tensor(parts[:, 1], whole, parts[:, 0].bitcast(F32), ALU.subtract))
                dve.wait_ge(mlp_in, 4 * DMA)
                raw1, raw2 = (raw_m[:, n].rearrange("p (k o t) -> p k o t", k=NBLOCKS, t=2) for n in range(2))
                top, bias = slice(0, BLOCK), slice(BLOCK, BLOCK + 1)
                for rows, at, t in ((top, 0, 0), (top, 2, 1), (bias, 1, 0), (bias, 2, 1)):
                    prep(nc.vector.tensor_copy(m1[rows, 0, :, at], raw1[rows, :, :, t]))
                    prep(nc.vector.tensor_tensor(m1[rows, 1, :, at], raw1[rows, :, :, t],
                                                 m1[rows, 0, :, at].bitcast(F32), ALU.subtract))
                for part in range(2):
                    prep(nc.vector.tensor_scalar(m1[top, part, :, 1], m1[top, part, :, 2].bitcast(F32),
                                                 -1.0, None, ALU.mult))
                for at, t in ((1, 0), (2, 1)):
                    prep(nc.vector.tensor_copy(m2[top, :, at], raw2[top, :, :, t]))
                    prep(nc.vector.tensor_scalar(m2[bias, :, at], raw2[bias, :, :, t], LAMBDA, None, ALU.add))
                prep(nc.vector.tensor_scalar(m2[top, :, 0], m2[top, :, 2], -1.0, None, ALU.mult))
                assert steps[0] == PREPARED

            def fold_w(k, o):
                if o == 0:
                    dve.wait_ge(pfold_done, k.count(1, 1))
                    if k.first >= BESIDE + 2:
                        dve.wait_ge(fwd_lo_done, k.count(4, -4 - 4 * BESIDE))
                    elif k.first >= 2:
                        dve.wait_ge(fwd_mm, k.count(4, -4))
                halves = [pf[:, :, v].rearrange("p f e c -> p f (e c)") for v in range(2)]
                nc.vector.tensor_tensor(wmov[:, k.slot, o], halves[0], halves[1],
                                        ALU.subtract if o else ALU.add).then_inc(wfold_done, 1)

            def fwd_step(k, tile):
                if tile % 2 and k.first + 1 < WUNITS:
                    fold_w(k + 1, tile // 2)

            def split_fwd(k, tile):
                dve.wait_ge(fwd_hi_done, k.count(4, tile + 1 - 4 * BESIDE))
                nc.vector.tensor_tensor(wmov_lo[:, tile % 2], wmov[:, k.slot, tile // 2, tile % 2],
                                        wmov_hi[:, tile % 2].bitcast(F32), ALU.subtract).then_inc(fwd_lo_done, 1)

            def split_inv(j, tile):
                dve.wait_ge(inv_hi_done, j.count(4, tile + 1))
                nc.vector.tensor_tensor(vmov_lo[:, tile % 2], vmov[:, j.slot, tile // 2, tile % 2],
                                        vmov_hi[:, tile % 2].bitcast(F32), ALU.subtract).then_inc(inv_lo_done, 1)

            def step(u, b):
                n = 2 * u.first + b
                if 3 <= n < STEPS + 3:
                    s = (n - 3) % 2
                    dve.wait_ge(above_done, u.count(2, b - 2))
                    if n >= 5:
                        dve.wait_ge(shr_lo_done, u.count(2, b - 4))
                    nc.vector.scalar_tensor_tensor(shrunk[:, s].rearrange("p e c -> p (e c)"), l2_bank[:, 0:PAIR],
                                                   0.0, above[:, s].rearrange("p e c -> p (e c)"),
                                                   ALU.min, ALU.add).then_inc(shrunk_done, 1)
                if n < STEPS:
                    dve.wait_ge(spec_hi_done, u.count(2, b + 1))
                    nc.vector.tensor_tensor(spec_lo[:, n % 2].rearrange("p t y -> p (t y)"), h_bank[b][0:BLOCK, :],
                                            spec_hi[0:BLOCK, n % 2].rearrange("p t y -> p (t y)").bitcast(F32),
                                            ALU.subtract).then_inc(spec_lo_done, 1)
                if 3 <= n < STEPS + 3:
                    dve.wait_ge(shr_hi_done, u.count(2, b - 2))
                    v, blk = (u - 1, 0) if b else (u - 2, 1)
                    nc.vector.tensor_tensor(shr_lo[:, v.slot, :, blk], shrunk[:, (n - 3) % 2],
                                            shr_hi[:, v.slot, :, blk].bitcast(F32),
                                            ALU.subtract).then_inc(shr_lo_done, 1)

            def unfold_w(j, form):
                dve.wait_ge(vev_done, j.count(2, form + 1))
                dve.wait_ge(inv_mm, j.count(4, 2 * form + 2))
                if form == 0 and j.first >= 1:
                    dve.wait_ge(vp_done, j.count(1, 0 if j.first <= ALONE else -1))
                odd, to = inv_bank(j, 2 * form + 1), vw_of(j)[form]
                nc.vector.tensor_tensor(to[:, 0:PAIR], vev[:, form], odd[:, 0:PAIR], ALU.add)
                nc.vector.tensor_tensor(to[:, PAIR:], vev[:, form], odd[:, 0:PAIR],
                                        ALU.subtract).then_inc(vw_done, 1)

            def unfold_h(j):
                dve.wait_ge(vp_done, j.count(1, 1))
                if j.first >= 2:
                    dve.wait_ge(y_put[j.slot], j.uses(0, 4))
                for hh in range(2):
                    nc.vector.tensor_tensor(yt[:, j.slot, :, hh], vp_of(j)[:, :, :, 0], vp_of(j)[:, :, :, 1],
                                            ALU.subtract if hh else ALU.add).then_inc(yt_rows, 1)

            def add_x(j):
                dve.wait_ge(yt_rows, j.count(2, 2))
                dve.wait_ge(xr_in[j.slot], j.uses(1, 4))
                rows = yt[:, j.slot].rearrange("p a h v c -> p (a h v c)")
                nc.vector.tensor_tensor(rows, rows, xr[:, j.slot].rearrange("p a h v c -> p (a h v c)"),
                                        ALU.add).then_inc(yt_done, 1)

            def inv_step(j, tile):
                if tile % 2 and j.first < WUNITS:
                    unfold_w(j, tile // 2)
                if tile == 2 and 1 <= j.first < WUNITS + 1:
                    unfold_h(j - 1)
                if tile == 0 and j.first >= 2:
                    add_x(j - 2)

            def unit(g, u, reg):
                for b in range(2):
                    step(Index(KX * g + u, reg, SPAN), b)
                    k, tile = forward_at(g, u, b, reg)
                    if k:
                        fwd_step(k, tile)
                    j, tile = inverse_at(g, u, b, reg)
                    if j:
                        inv_step(j, tile)
                    k, tile = forward_at(g, u, b, reg, late=0)
                    if k and k.first < WUNITS:
                        split_fwd(k, tile)
                    j, tile = inverse_at(g, u, b, reg, late=0)
                    if j:
                        split_inv(j, tile)

            def fwd_alone(k):
                for tile in range(4):
                    fwd_step(k, tile)
                    if tile == 0:
                        fold_h(dve, nc.vector, k + 2, 1)
                fold_p(dve, nc.vector, k + 2)

            def inv_alone(j):
                for tile in range(4):
                    inv_step(j, tile)

            prepare_ones()
            fold_h(dve, nc.vector, Index(0), 1)
            fold_p(dve, nc.vector, Index(0))
            for o in range(2):
                fold_w(Index(0), o)
            fold_h(dve, nc.vector, Index(1), 1)
            fold_p(dve, nc.vector, Index(1))
            prepare()
            walk_w(dve, fwd_alone, 0, 2, QUAD - 2, BESIDE)
            walk(dve, unit)
            walk_w(dve, inv_alone, ALONE, ALONE + 2, WUNITS, WUNITS + 2)

        @block.gpsimd
        def _(pool):
            def unfold_p(j):
                pool.wait_ge(vw_done, j.count(2, 2))
                if j.first >= 1:
                    pool.wait_ge(yt_rows, j.count(2, 0 if j.first <= ALONE else -2))
                source, to = vw_of(j), vp_of(j)
                if j.first % QUAD == 0:
                    for pair in range(2):
                        last = nc.gpsimd.tensor_copy(to[:, pair].rearrange("p v e c -> p (v e c)"), source[pair])
                else:
                    c, s = (part.rearrange("p (v e c) -> p v e c", v=2, e=2) for part in source)
                    nc.gpsimd.tensor_tensor(to[:, 0].rearrange("p v e c -> p (v e c)"), *source, ALU.add)
                    nc.gpsimd.tensor_tensor(to[:, 1, :, 0], c[:, :, 0], s[:, :, 0], ALU.subtract)
                    last = nc.gpsimd.tensor_tensor(to[:, 1, :, 1], s[:, :, 1], c[:, :, 1], ALU.subtract)
                last.then_inc(vp_done, 1)

            def unit(g, u, reg):
                for b in range(2):
                    k, tile = forward_at(g, u, b, reg)
                    if k and tile == 0 and k.first + 2 < WUNITS:
                        for pair in range(2):
                            fold_h(pool, nc.gpsimd, k + 2, pair)
                    j, inv_tile = inverse_at(g, u, b, reg)
                    if j and inv_tile == 3:
                        unfold_p(j)
                    if k and tile == 3 and k.first + 2 < WUNITS:
                        fold_p(pool, nc.gpsimd, k + 2)

            walk_w(pool, lambda k: fold_h(pool, nc.gpsimd, k, 0), 0, 2, BESIDE, BESIDE + 2)
            walk(pool, unit)
            walk_w(pool, unfold_p, ALONE, ALONE + 2, WUNITS, WUNITS)


PREPARED = 23


def dft_constants():
    def twelve(v):
        m, e = np.frexp(v)
        return np.ldexp(np.rint(m * 4096.0) / 4096.0, e)

    def parts(a):
        hi = twelve(a)
        return np.ascontiguousarray(np.stack([hi, twelve(a - hi)], axis=1).astype(np.float32))

    i = np.arange(HALF)
    scale = 1.0 / np.sqrt(SIDE)
    fwd_w, inv_w = np.zeros((HALF, 2, 128)), np.zeros((128, 2, 2, HALF))
    fwd_h, inv_h = np.zeros((128, 2, 4, HALF)), np.zeros((HALF, 2, 128))
    row = np.arange(128)
    for parity in range(2):
        angle = 2 * np.pi * (np.outer(i, 2 * i + parity) % SIDE) / SIDE
        cos, sin = scale * np.cos(angle), scale * np.sin(angle)
        k = QUAD
        fwd_w[:, parity, :k], fwd_w[:, parity, k:] = cos[:, :k], -sin[:, :k]
        inv_w[:k, 0, parity], inv_w[k:, 0, parity] = 2 * cos[:, :k].T, -2 * sin[:, :k].T
        at = np.where(row > 64, row - 64, row)
        is_cos = (row < 64) | ((row == 64) & (parity == 0))
        c, s = cos[at] * is_cos[:, None], sin[at] * ~is_cos[:, None]
        fwd_h[:, parity, 0], fwd_h[:, parity, 1], fwd_h[:, parity, 2], fwd_h[:, parity, 3] = c + s, c - s, c, -s
        inv_h[:, parity] = (c + s).T
    nyquist = scale * (1.0 - 2.0 * (i % 2))
    fwd_w[:, 0, 64] = nyquist
    inv_w[0, 0, 0], inv_w[64, 0, 0] = scale, nyquist
    inv_w[:, 1] = inv_w[:, 0]
    inv_w[0:64, 1] *= -1.0
    inv_w[64, 1, 0] *= -1.0
    return (fwd_w.astype(np.float32), inv_w.astype(np.float32), fwd_h.astype(np.float32),
            parts(inv_h).reshape(128, -1))


def kernel(**inputs):
    import concourse.bacc as bacc
    from concourse.bass_utils import run_bass_kernel_spmd

    nc = bacc.Bacc("TRN2", target_bir_lowering=False, num_devices=1)
    fwd_w, inv_w, fwd_h, inv_h = dft_constants()
    arrays = {name: np.ascontiguousarray(inputs[name]) for name in
              ("x", "L0_conv_w1", "L0_conv_b1", "L0_conv_w2", "L0_conv_b2")}
    arrays.update(fwd_w=fwd_w, inv_w=inv_w, fwd_h=fwd_h, inv_h=inv_h)
    args = [nc.dram_tensor("in_" + name, a.shape, mybir.dt.from_np(a.dtype), kind="ExternalInput").ap()
            for name, a in arrays.items()]
    out = nc.dram_tensor("out_dram", arrays["x"].shape, F32, kind="ExternalOutput").ap()
    spectral_conv(nc, *args, out)
    result = run_bass_kernel_spmd(nc, [{"in_" + name: a for name, a in arrays.items()}], core_ids=[0])
    return result.results[0]["out_dram"]
```
